# Optimizing a Trainium2 kernel written in Bass

```python
import numpy as np
import jax
import jax.numpy as jnp

def _softmax(x, axis=-1):
    return jax.nn.softmax(x, axis=axis)

def _gelu(x):
    return jax.nn.gelu(x, approximate=True)

def _silu(x):
    return jax.nn.silu(x)

def _sigmoid(x):
    return jax.nn.sigmoid(x)

def _layernorm(x, axis=-1, eps=1e-05):
    m = jnp.mean(x, axis=axis, keepdims=True)
    v = jnp.var(x, axis=axis, keepdims=True)
    return (x - m) / jnp.sqrt(v + eps)

def _scatter_add(tgt, idx, src, axis=0):
    return tgt.at[idx].add(src)

def _segment_sum(src, seg, n):
    return jax.ops.segment_sum(src, seg, n)
kernel_name = 'mk_gnn_resnorm_d4_gnn_r32_76701a'

def setup_inputs(seed: int=0):
    np.random.seed(seed)
    _w = jnp.asarray

    def _rec_inputs():
        import jax
        import jax.numpy as jnp
        _gk = jax.random.key(seed)
        x = -0.0003713 + 1 * jax.random.normal(jax.random.fold_in(_gk, 1), (3125, 128), jnp.float32)
        src = jax.random.randint(jax.random.fold_in(_gk, 2), (100000,), 0, 3125, jnp.int32)
        dst = jax.random.randint(jax.random.fold_in(_gk, 3), (100000,), 0, 3125, jnp.int32)
        _o = jnp.argsort(dst, stable=True)
        src = src[_o]
        dst = dst[_o]
        edge_weight = jax.random.uniform(jax.random.fold_in(_gk, 13), (100000,), jnp.float32, 0.0, 1)
        return (x, src, dst, edge_weight)
    x, src, dst, edge_weight = _rec_inputs()

    def _L0_gnn_setup():
        import jax, jax.numpy as jnp
        import numpy as np
        N = 3125
        E = 100000
        D_IN = 128
        D_OUT = 128
        key = jax.random.key(seed)
        k1, k2, k3, k4, k5, k6 = jax.random.split(key, 6)
        x = jax.random.normal(k1, (N, D_IN), dtype=jnp.float32)
        edge_row = jax.random.randint(k2, (E,), 0, N)
        edge_col = jax.random.randint(k3, (E,), 0, N)
        edge_val = jax.random.uniform(k4, (E,), dtype=jnp.float32)
        stdv = 1.0 / np.sqrt(D_OUT)
        weight = jax.random.uniform(k5, (D_IN, D_OUT), dtype=jnp.float32, minval=-stdv, maxval=stdv)
        bias = jax.random.uniform(k6, (D_OUT,), dtype=jnp.float32, minval=-stdv, maxval=stdv)
        return {'x': x, 'edge_row': edge_row, 'edge_col': edge_col, 'edge_val': edge_val, 'weight': weight, 'bias': bias}
    _L0_gnn_all = _L0_gnn_setup()
    _L0_gnn_in = {k: v for k, v in _L0_gnn_all.items() if k in ('weight', 'bias')}
    del _L0_gnn_all

    def _L1_gnn_setup():
        import jax, jax.numpy as jnp
        import numpy as np
        N_NODES = 3125
        N_EDGES = 18750
        DIM = 128
        key = jax.random.key(seed)
        k = jax.random.split(key, 6)
        h = jax.random.normal(k[0], (N_NODES, DIM), dtype=jnp.float32)
        edge_index = jax.random.randint(k[1], (2, N_EDGES), 0, N_NODES, dtype=jnp.int64)
        s = 1.0 / np.sqrt(DIM)
        W_self = jax.random.normal(k[2], (DIM, DIM), dtype=jnp.float32) * s
        b_self = jax.random.normal(k[3], (DIM,), dtype=jnp.float32) * s
        W_nei = jax.random.normal(k[4], (DIM, DIM), dtype=jnp.float32) * s
        b_nei = jax.random.normal(k[5], (DIM,), dtype=jnp.float32) * s
        return {'h': h, 'edge_index': edge_index, 'W_self': W_self, 'b_self': b_self, 'W_nei': W_nei, 'b_nei': b_nei}
    _L1_gnn_all = _L1_gnn_setup()
    _L1_gnn_in = {k: v for k, v in _L1_gnn_all.items() if k in ('W_self', 'b_self', 'W_nei', 'b_nei')}
    del _L1_gnn_all

    def _L2_gnn_setup():
        import jax, jax.numpy as jnp
        import numpy as np
        N_NODES = 50000
        N_EDGES = 25000
        D_IN = 128
        D_EMB = 128
        D_HID = 2 * D_EMB
        key = jax.random.key(seed)
        ks = jax.random.split(key, 9)
        x = jax.random.normal(ks[0], (N_NODES, D_IN), dtype=jnp.float32)
        edge_index = jax.random.randint(ks[1], (2, N_EDGES), 0, N_NODES, dtype=jnp.int32)
        s = 1.0 / np.sqrt(D_IN)
        W_l = jax.random.uniform(ks[2], (D_IN, D_HID), jnp.float32, -s, s)
        b_l = jax.random.uniform(ks[3], (D_HID,), jnp.float32, -s, s)
        W_r = jax.random.uniform(ks[4], (D_IN, D_HID), jnp.float32, -s, s)
        sh = 1.0 / np.sqrt(D_HID)
        Wm1 = jax.random.uniform(ks[5], (D_HID, D_HID), jnp.float32, -sh, sh)
        bm1 = jax.random.uniform(ks[6], (D_HID,), jnp.float32, -sh, sh)
        Wm2 = jax.random.uniform(ks[7], (D_HID, D_EMB), jnp.float32, -sh, sh)
        bm2 = jax.random.uniform(ks[8], (D_EMB,), jnp.float32, -sh, sh)
        return {'x': x, 'edge_index': edge_index, 'W_l': W_l, 'b_l': b_l, 'W_r': W_r, 'Wm1': Wm1, 'bm1': bm1, 'Wm2': Wm2, 'bm2': bm2}
    _L2_gnn_all = _L2_gnn_setup()
    _L2_gnn_in = {k: v for k, v in _L2_gnn_all.items() if k in ('W_l', 'b_l', 'W_r', 'Wm1', 'bm1', 'Wm2', 'bm2')}
    del _L2_gnn_all

    def _L3_gnn_setup():
        import jax, jax.numpy as jnp
        import numpy as np
        ALPHA = 0.2
        LN_EPS = 1e-05
        N_NODES = 3125
        N_EDGES = 50000
        F_IN = 128
        F_OUT = 128
        key = jax.random.key(seed)
        k_x, k_e, k_w, k_a = jax.random.split(key, 4)
        x = jax.random.normal(k_x, (N_NODES, F_IN), dtype=jnp.float32)
        edge = jax.random.randint(k_e, (2, N_EDGES), 0, N_NODES, dtype=jnp.int64)
        std_w = 1.414 * np.sqrt(2.0 / (F_IN + F_OUT))
        W = jax.random.normal(k_w, (F_IN, F_OUT), dtype=jnp.float32) * std_w
        std_a = 1.414 * np.sqrt(2.0 / (1 + 2 * F_OUT))
        a = jax.random.normal(k_a, (2 * F_OUT,), dtype=jnp.float32) * std_a
        bias = jnp.zeros((F_OUT,), dtype=jnp.float32)
        gamma = jnp.ones((F_OUT,), dtype=jnp.float32)
        beta = jnp.zeros((F_OUT,), dtype=jnp.float32)
        return {'input': x, 'edge': edge, 'W': W, 'a': a, 'bias': bias, 'gamma': gamma, 'beta': beta}
    _L3_gnn_all = _L3_gnn_setup()
    _L3_gnn_in = {k: v for k, v in _L3_gnn_all.items() if k in ('W', 'a', 'bias', 'gamma', 'beta')}
    del _L3_gnn_all
    return {'x': x, 'src': src, 'dst': dst, 'edge_weight': edge_weight, 'L0_gnn_weight': _L0_gnn_in['weight'], 'L0_gnn_bias': _L0_gnn_in['bias'], 'L1_gnn_W_self': _L1_gnn_in['W_self'], 'L1_gnn_b_self': _L1_gnn_in['b_self'], 'L1_gnn_W_nei': _L1_gnn_in['W_nei'], 'L1_gnn_b_nei': _L1_gnn_in['b_nei'], 'L2_gnn_W_l': _L2_gnn_in['W_l'], 'L2_gnn_b_l': _L2_gnn_in['b_l'], 'L2_gnn_W_r': _L2_gnn_in['W_r'], 'L2_gnn_Wm1': _L2_gnn_in['Wm1'], 'L2_gnn_bm1': _L2_gnn_in['bm1'], 'L2_gnn_Wm2': _L2_gnn_in['Wm2'], 'L2_gnn_bm2': _L2_gnn_in['bm2'], 'L3_gnn_W': _L3_gnn_in['W'], 'L3_gnn_a': _L3_gnn_in['a'], 'L3_gnn_bias': _L3_gnn_in['bias'], 'L3_gnn_gamma': _L3_gnn_in['gamma'], 'L3_gnn_beta': _L3_gnn_in['beta']}

def reference(x, src, dst, edge_weight, L0_gnn_weight, L0_gnn_bias, L1_gnn_W_self, L1_gnn_b_self, L1_gnn_W_nei, L1_gnn_b_nei, L2_gnn_W_l, L2_gnn_b_l, L2_gnn_W_r, L2_gnn_Wm1, L2_gnn_bm1, L2_gnn_Wm2, L2_gnn_bm2, L3_gnn_W, L3_gnn_a, L3_gnn_bias, L3_gnn_gamma, L3_gnn_beta):
    import jax
    import jax.numpy as jnp

    def _L0_gnn_ref(x, edge_row, edge_col, edge_val, weight, bias):
        import jax, jax.numpy as jnp
        import numpy as np
        N = 3125
        E = 100000
        D_IN = 128
        D_OUT = 128
        support = x @ weight
        msgs = support[edge_col] * edge_val[:, None]
        out = jax.ops.segment_sum(msgs, edge_row, num_segments=N)
        return out + bias

    def _L1_gnn_ref(h, edge_index, W_self, b_self, W_nei, b_nei):
        import jax, jax.numpy as jnp
        import numpy as np
        N_NODES = 3125
        N_EDGES = 18750
        DIM = 128
        src, dst = (edge_index[0], edge_index[1])
        n = h.shape[0]
        msgs = h[src]
        agg = jax.ops.segment_sum(msgs, dst, num_segments=n)
        deg = jax.ops.segment_sum(jnp.ones_like(dst, dtype=h.dtype), dst, num_segments=n)
        deg = jnp.clip(deg, 1.0, None)[:, None]
        mean = agg / deg
        out = h @ W_self.T + b_self + mean @ W_nei.T + b_nei
        return jax.nn.relu(out)

    def _L2_gnn_ref(x, edge_index, W_l, b_l, W_r, Wm1, bm1, Wm2, bm2):
        import jax, jax.numpy as jnp
        import numpy as np
        N_NODES = 50000
        N_EDGES = 25000
        D_IN = 128
        D_EMB = 128
        D_HID = 2 * D_EMB
        n = x.shape[0]
        src, dst = (edge_index[0], edge_index[1])
        msg = x[src]
        agg_sum = jax.ops.segment_sum(msg, dst, num_segments=n)
        deg = jax.ops.segment_sum(jnp.ones((src.shape[0],), x.dtype), dst, num_segments=n)
        agg = agg_sum / jnp.maximum(deg, 1.0)[:, None]
        h = jax.nn.relu(agg @ W_l + x @ W_r + b_l)
        h = jax.nn.relu(h @ Wm1 + bm1)
        return h @ Wm2 + bm2

    def _L3_gnn_ref(input, edge, W, a, bias, gamma, beta):
        import jax, jax.numpy as jnp
        import numpy as np
        ALPHA = 0.2
        LN_EPS = 1e-05
        N_NODES = 3125
        N_EDGES = 50000
        F_IN = 128
        F_OUT = 128
        N = input.shape[0]
        F = W.shape[1]
        src, dst = (edge[0], edge[1])
        h = input @ W + bias
        s_src = h @ a[:F]
        s_dst = h @ a[F:]
        e = jax.nn.leaky_relu(s_src[src] + s_dst[dst], ALPHA)
        e = jnp.exp(e - jnp.max(e))
        rowsum = jax.ops.segment_sum(e, src, num_segments=N) + 1e-08
        h_prime = jax.ops.segment_sum(e[:, None] * h[dst], src, num_segments=N)
        h_prime = h_prime / rowsum[:, None]
        h_prime = h_prime + input
        mu = jnp.mean(h_prime, axis=-1, keepdims=True)
        var = jnp.var(h_prime, axis=-1, keepdims=True)
        h_norm = (h_prime - mu) / jnp.sqrt(var + LN_EPS) * gamma + beta
        return jax.nn.elu(h_norm)
    edge_index = jnp.stack([src, dst])
    x = _layernorm(x + _L0_gnn_ref(x, src, dst, edge_weight, L0_gnn_weight, L0_gnn_bias), axis=-1)
    x = _layernorm(x + _L1_gnn_ref(x, edge_index, L1_gnn_W_self, L1_gnn_b_self, L1_gnn_W_nei, L1_gnn_b_nei), axis=-1)
    x = _layernorm(x + _L2_gnn_ref(x, edge_index, L2_gnn_W_l, L2_gnn_b_l, L2_gnn_W_r, L2_gnn_Wm1, L2_gnn_bm1, L2_gnn_Wm2, L2_gnn_bm2), axis=-1)
    x = _layernorm(x + _L3_gnn_ref(x, edge_index, L3_gnn_W, L3_gnn_a, L3_gnn_bias, L3_gnn_gamma, L3_gnn_beta), axis=-1)
    return x

_drawn_inputs = setup_inputs


def setup_inputs(seed=0):
    import zlib

    import numpy as np

    out = dict(_drawn_inputs(seed))
    spreads = {'L3_gnn_bias': (0.0, 0.1), 'L3_gnn_gamma': (1.0, 0.2), 'L3_gnn_beta': (0.0, 0.1)}
    factors = {'L2_gnn_b_l': 6.994, 'L2_gnn_bm1': 3.501}
    for name, (base, spread) in spreads.items():
        noise = np.random.default_rng([zlib.crc32(name.encode()), seed]).standard_normal(out[name].shape)
        drawn = base * np.exp(spread * noise) if base else spread * noise
        out[name] = jnp.asarray(drawn.astype(out[name].dtype))
    for name, factor in factors.items():
        out[name] = (out[name] * factor).astype(out[name].dtype)
    return out
```

```python
from contextlib import ExitStack

import concourse.bass as bass
from concourse import mybir

ALU = mybir.AluOpType
ACT = mybir.ActivationFunctionType
AX_X = mybir.AxisListType.X
F32 = mybir.dt.float32
I32 = mybir.dt.int32
RMAX = bass.bass_isa.ReduceOp.max

LN_EPS = 1e-5
ALPHA = 0.2
SUM_EPS = 1e-8


def gnn_stack(nc, x_in, src, dst, edge_weight, w0, b0, w_selfT, b_self, w_neiT, b_nei,
              w_l, b_l, w_r, wm1, bm1, wm2, bm2, w3, a3, b3, gamma, beta, out):
    N, D = x_in.shape
    E = src.shape[0]
    P = 125
    H = N // P
    EC = E // P
    QB = 4
    QW = QB * P
    GROUPS = [(q * QW, min(QW, N - q * QW)) for q in range(-(-N // QW))]
    NQ = len(GROUPS)
    BLOCKS = [list(range(q * QB, min(H, (q + 1) * QB))) for q in range(NQ)]
    assert H * P == N and EC * P == E and EC % 2 == 0 and D == 128
    HALVES = w_l.shape[1] // D

    with ExitStack() as ctx:
        def sb(name, shape, dt=F32):
            return ctx.enter_context(nc.sbuf_tensor(name, shape, dt))

        def sem(name):
            return ctx.enter_context(nc.semaphore(name))

        acc = ctx.enter_context(nc.psum_tensor("acc", [128, 8, 512], F32))

        x = sb("x", [P, H, D])
        xT = sb("xT", [128, N])
        aggT = sb("aggT", [128, N])
        normT = sb("normT", [128, N])
        yT = sb("yT", [128, N])
        hidden = sb("hidden", [128, HALVES, N])
        x3 = sb("x3", [P, H, D])
        hid2 = [aggT, yT]
        src_i = sb("src_i", [P, EC], I32)
        dst_i = sb("dst_i", [P, EC], I32)
        src_f = sb("src_f", [P, EC])
        dst_f = sb("dst_f", [P, EC])
        w_e = sb("w_e", [P, EC])
        ones_e = sb("ones_e", [P, EC])
        s_of = [sb("s_of_dst", [P, EC]), sb("s_of_src", [P, EC])]
        node_iota = sb("node_iota", [P, N])
        ident = sb("ident", [128, 128])
        ones = sb("ones", [128, 128])
        zeros = sb("zeros", [P, 512])
        eps = sb("eps", [128, 1])
        W0, WS, WN, W3 = sb("W0", [D, D]), sb("WS", [D, D]), sb("WN", [D, D]), sb("W3", [D, D])
        WL, WR = sb("WL", [D, HALVES * D]), sb("WR", [D, HALVES * D])
        WM1 = sb("WM1", [D, HALVES, HALVES * D])
        WM2 = sb("WM2", [D, HALVES, D])
        A3 = sb("A3", [D, 2])
        B0, BS, BN_, B3, G3, BE3, BM2 = (sb(n, [D, 1]) for n in ("B0", "BS", "BN", "B3", "G3", "BE3", "BM2"))
        BL, BM1 = sb("BL", [D, HALVES]), sb("BM1", [D, HALVES])
        gidx = [sb(f"gidx{s}", [P, 1], I32) for s in range(2)]
        rows = [sb(f"rows{s}", [P, D]) for s in range(2)]
        srow = [sb(f"srow{s}", [P, 2]) for s in range(2)]
        msg = [sb(f"msg{s}", [P, D]) for s in range(2)]
        onehot = [sb(f"onehot{s}", [P, N]) for s in range(2)]
        stats = sb("stats", [P, H, 6])
        mv = sb("mv", [P, H, 2])
        rstd = sb("rstd", [P, H])
        s_node = sb("s_node", [P, H, 2])
        z_e = sb("z_e", [P, EC])
        e_e = sb("e_e", [P, EC])
        pmax = sb("pmax", [P, 1])
        pause = sb("pause", [P, 1])
        gmax = sb("gmax", [P, 1])
        tmp = sb("tmp", [128, QW])
        tmp2 = sb("tmp2", [128, QW])

        tables = [x_in] + [nc.dram_tensor(f"x{n}_tab", [N, D], F32, kind="Internal").ap() for n in (1, 2, 3)]
        s_table = nc.dram_tensor("s_tab", [N, 2], F32, kind="Internal").ap()

        loaded = sem("loaded")
        consts_ready = sem("consts_ready")
        dve_chain = sem("dve_chain")
        edges_ready = sem("edges_ready")
        gidx_ready = sem("gidx_ready")
        gathered = [sem(f"gathered{s}") for s in range(2)]
        sgathered = [sem(f"sgathered{s}") for s in range(2)]
        scol_done = sem("scol_done")
        msg_ready = sem("msg_ready")
        chunk_done = sem("chunk_done")
        scatter_done = sem("scatter_done")
        agg_out = sem("agg_out")
        mm_done = sem("mm_done")
        ev_dve = sem("ev_dve")
        ev_act = sem("ev_act")
        var_ready = sem("var_ready")
        std_ready = sem("std_ready")
        elu_in = sem("elu_in")
        elu_exp = sem("elu_exp")
        x_new = sem("x_new")
        table_ready = sem("table_ready")
        s_tab_ready = sem("s_tab_ready")
        exp_in = sem("exp_in")
        exp_out = sem("exp_out")
        max_in = sem("max_in")
        max_out = sem("max_out")
        out_ready = sem("out_ready")
        out_stored = sem("out_stored")

        ROUNDS = [("fwd0", ev_dve),
                  ("lin0", ev_dve), ("back0", ev_dve), ("fwd1", ev_dve),
                  ("lin1", ev_act), ("back1", ev_dve), ("fwd2", ev_dve),
                  ("l2h0", ev_act), ("l2h1", ev_act), ("l2m0", ev_act), ("l2m1", ev_act), ("l2o", ev_dve),
                  ("back2", ev_dve), ("fwd3", ev_dve),
                  ("h3", ev_dve), ("s3", ev_dve),
                  ("lin3", ev_dve), ("back3", ev_dve), ("fwd3n", ev_dve), ("back4", ev_dve)]
        NUMBER = {name: n for n, (name, _) in enumerate(ROUNDS)}

        def filled(name, q):
            return NQ * NUMBER[name] + q + 1

        def emptied(name, q):
            n = NUMBER[name]
            same = sum(1 for _, s in ROUNDS[:n] if s is ROUNDS[n][1])
            return ROUNDS[n][1], NQ * same + q + 1

        PASSES = ["agg0", "deg", "agg1", "agg2", "rowsum", "agg3"]
        GATHERS = [p for p in PASSES if p.startswith("agg")]

        NLOAD = 4
        loads = [(x[:], x_in.rearrange("(h p) d -> p h d", p=P)),
                 (src_i[:], src.rearrange("(p c) -> p c", p=P)),
                 (dst_i[:], dst.rearrange("(p c) -> p c", p=P)),
                 (w_e[:], edge_weight.rearrange("(p c) -> p c", p=P)),
                 (W0[:], w0), (WS[:], w_selfT), (WN[:], w_neiT), (W3[:], w3), (WL[:], w_l), (WR[:], w_r),
                 (WM1[:], wm1.rearrange("(k p) n -> p k n", p=D)),
                 (WM2[:], wm2.rearrange("(k p) n -> p k n", p=D)),
                 (A3[:], a3.rearrange("(k p) -> p k", p=D)),
                 (BL[:], b_l.rearrange("(k p) -> p k", p=D)),
                 (BM1[:], bm1.rearrange("(k p) -> p k", p=D)),
                 ] + [(t[:], v.rearrange("(p k) -> p k", k=1)) for t, v in
                      ((B0, b0), (BS, b_self), (BN_, b_nei), (B3, b3), (G3, gamma), (BE3, beta), (BM2, bm2))]

        block = ctx.enter_context(nc.Block())

        @block.sync
        def _(sp):
            with nc.allow_non_contiguous_dma(reason="a bias per feature: 128 short runs each"):
                for to, frm in loads:
                    sp.dma_start(to, frm).then_inc(loaded, 16)
            for layer in (1, 2, 3):
                sp.wait_ge(x_new, layer)
                sp.dma_start(tables[layer].rearrange("(h p) d -> p h d", p=P), x[:]).then_inc(table_ready, 16)
            sp.wait_ge(emptied("s3", NQ - 1)[0], emptied("s3", NQ - 1)[1])
            sp.dma_start(s_table.rearrange("(h p) k -> p h k", p=P), s_node[:]).then_inc(s_tab_ready, 16)
            sp.wait_ge(x_new, 4)
            sp.dma_start(out.rearrange("(h p) d -> p h d", p=P), x[:]).then_inc(out_stored, 16)
            sp.wait_ge(out_stored, 16)
            sp.wait_ge(table_ready, 48)
            sp.wait_ge(s_tab_ready, 16)

        @block.gpsimd
        def _(pool):
            nc.gpsimd.iota(node_iota[:], [[1, N]], base=0, channel_multiplier=0,
                           allow_small_or_imprecise_dtypes=True).then_inc(consts_ready, 1)
            nc.gpsimd.memset(ident[:], 0.0).then_inc(consts_ready, 1)
            pool.wait_ge(consts_ready, 2)
            nc.gpsimd.affine_select(out=ident[:], in_=ident[:], compare_op=ALU.not_equal, fill=1.0, base=0,
                                    pattern=[[-1, 128]], channel_multiplier=1).then_inc(consts_ready, 1)
            pool.wait_ge(loaded, 16 * len(loads))
            n_idx = [0]

            def gather_rows(name, idx, table):
                p, g = PASSES.index(name), GATHERS.index(name)
                with pool.Fori(0, EC // 2) as i:
                    for s in range(2):
                        pool.wait_ge(chunk_done, (EC + 2) * p + i * 2 + s + 1)
                        nc.gpsimd.tensor_copy(gidx[s][:], idx[:, bass.ds(i * 2 + s, 1)]).then_inc(gidx_ready, 1)
                        pool.wait_ge(gidx_ready, n_idx[0] + i * 2 + s + 1)
                        nc.gpsimd.tensor_tensor(pause[:], ident[0:P, 0:1], ident[0:P, 0:1], ALU.add)
                        nc.gpsimd.indirect_dma_start(
                            out=rows[s][:], out_offset=None, in_=table,
                            in_offset=bass.IndirectOffsetOnAxis(gidx[s][:, 0:1], 0)).then_inc(gathered[s], 16)
                n_idx[0] += EC

            gather_rows("agg0", dst_i, tables[0])
            pool.wait_ge(table_ready, 16)
            gather_rows("agg1", src_i, tables[1])
            pool.wait_ge(table_ready, 32)
            gather_rows("agg2", src_i, tables[2])
            pool.wait_ge(s_tab_ready, 16)
            for k, idx in enumerate((dst_i, src_i)):
                with pool.Fori(0, EC // 2) as i:
                    for s in range(2):
                        pool.wait_ge(scol_done, EC * k + i * 2 + s + 1)
                        nc.gpsimd.tensor_copy(gidx[s][:], idx[:, bass.ds(i * 2 + s, 1)]).then_inc(gidx_ready, 1)
                        pool.wait_ge(gidx_ready, n_idx[0] + i * 2 + s + 1)
                        nc.gpsimd.tensor_tensor(pause[:], ident[0:P, 0:1], ident[0:P, 0:1], ALU.add)
                        nc.gpsimd.indirect_dma_start(
                            out=srow[s][:], out_offset=None, in_=s_table,
                            in_offset=bass.IndirectOffsetOnAxis(gidx[s][:, 0:1], 0)).then_inc(sgathered[s], 16)
                n_idx[0] += EC
            pool.wait_ge(max_in, 1)
            nc.gpsimd.partition_all_reduce(gmax[:], pmax[:], P, RMAX).then_inc(max_out, 1)
            pool.wait_ge(table_ready, 48)
            gather_rows("agg3", dst_i, tables[3])

        @block.tensor
        def _(pe):
            def scatter(name):
                p = PASSES.index(name)
                for q, (c0, cw) in enumerate(GROUPS):
                    last = nc.tensor.matmul(acc[:, q, 0:cw], zeros[:, 0:D], zeros[:, 0:cw], start=True, stop=False)
                last.then_inc(chunk_done, 2)
                with pe.Fori(0, EC // 2) as i:
                    for s in range(2):
                        pe.wait_ge(msg_ready, EC * p + i * 2 + s + 1)
                        for q, (c0, cw) in enumerate(GROUPS):
                            last = nc.tensor.matmul(acc[:, q, 0:cw], msg[s][:], onehot[s][:, c0:c0 + cw],
                                                    start=False, stop=False)
                        last.then_inc(chunk_done, 1)
                for q, (c0, cw) in enumerate(GROUPS):
                    nc.tensor.matmul(acc[:, q, 0:cw], zeros[:, 0:D], zeros[:, 0:cw],
                                     start=False, stop=True).then_inc(scatter_done, 1)

            def fill(name, steps):
                before = ROUNDS[NUMBER[name] - 1][0] if NUMBER[name] else None
                for q, (c0, cw) in enumerate(GROUPS):
                    if before:
                        pe.wait_ge(*emptied(before, q))
                    steps(q, c0, cw).then_inc(mm_done, 1)

            def to_nodes(name, frm):
                def steps(q, c0, cw):
                    for j, b in enumerate(BLOCKS[q]):
                        last = nc.tensor.transpose(acc[0:P, q, j * D:(j + 1) * D], frm[:, b * P:(b + 1) * P], ident[:])
                    return last
                fill(name, steps)

            def to_features(name, frm):
                def steps(q, c0, cw):
                    for j, b in enumerate(BLOCKS[q]):
                        last = nc.tensor.transpose(acc[:, q, j * P:(j + 1) * P], frm[:, b, :], ident[0:P, 0:P])
                    return last
                fill(name, steps)

            def linear(name, terms):
                def steps(q, c0, cw):
                    for n, (w, v) in enumerate(terms):
                        last = nc.tensor.matmul(acc[:, q, 0:cw], w, v[:, c0:c0 + cw],
                                                start=(n == 0), stop=(n == len(terms) - 1))
                    return last
                fill(name, steps)

            pe.wait_ge(loaded, 16 * len(loads))
            pe.wait_ge(consts_ready, 3)
            pe.wait_ge(edges_ready, 1)
            to_features("fwd0", x)
            pe.wait_ge(*emptied("fwd0", NQ - 1))
            scatter("agg0")
            pe.wait_ge(agg_out, NQ)
            linear("lin0", [(W0[:], aggT)])
            to_nodes("back0", yT)
            to_features("fwd1", x)
            pe.wait_ge(*emptied("fwd1", NQ - 1))
            scatter("deg")
            pe.wait_ge(agg_out, 2 * NQ)
            scatter("agg1")
            pe.wait_ge(agg_out, 3 * NQ)
            linear("lin1", [(WS[:], xT), (WN[:], aggT)])
            pe.wait_ge(ev_act, NQ)
            pe.wait_ge(elu_in, NQ)
            to_nodes("back1", yT)
            to_features("fwd2", x)
            pe.wait_ge(*emptied("fwd2", NQ - 1))
            scatter("agg2")
            pe.wait_ge(agg_out, 4 * NQ)
            for k in range(HALVES):
                c = slice(k * D, (k + 1) * D)
                linear(f"l2h{k}", [(WL[:, c], aggT), (WR[:, c], xT)])
            for k in range(HALVES):
                c = slice(k * D, (k + 1) * D)
                linear(f"l2m{k}", [(WM1[:, j, c], hidden[:, j]) for j in range(HALVES)])
            linear("l2o", [(WM2[:, j, :], hid2[j]) for j in range(HALVES)])
            to_nodes("back2", yT)
            to_features("fwd3", x)
            linear("h3", [(W3[:], xT)])

            def node_terms(q, c0, cw):
                for j, b in enumerate(BLOCKS[q]):
                    last = nc.tensor.matmul(acc[0:P, q, 2 * j:2 * j + 2], hidden[:, 0, b * P:(b + 1) * P], A3[:],
                                            start=True, stop=True)
                return last
            fill("s3", node_terms)
            pe.wait_ge(*emptied("s3", NQ - 1))
            scatter("rowsum")
            pe.wait_ge(agg_out, 5 * NQ)
            scatter("agg3")
            pe.wait_ge(agg_out, 6 * NQ)
            linear("lin3", [(W3[:], aggT)])
            to_nodes("back3", yT)
            to_features("fwd3n", x3)
            to_nodes("back4", yT)

        @block.scalar
        def _(act):
            def roots(n):
                act.wait_ge(var_ready, n)
                nc.scalar.activation(rstd[:], mv[:, :, 1], ACT.Sqrt, bias=eps[0:P, :]).then_inc(std_ready, 1)

            def relus(name, to, bias):
                for q, (c0, cw) in enumerate(GROUPS):
                    act.wait_ge(mm_done, filled(name, q))
                    nc.scalar.activation(to[:, c0:c0 + cw], acc[:, q, 0:cw], ACT.Relu, bias=bias).then_inc(ev_act, 1)

            roots(1)
            relus("lin1", yT, BS[:])
            roots(2)
            for k in range(HALVES):
                relus(f"l2h{k}", hidden[:, k], BL[:, k:k + 1])
            for k in range(HALVES):
                relus(f"l2m{k}", hid2[k], BM1[:, k:k + 1])
            roots(3)
            act.wait_ge(exp_in, 1)
            nc.scalar.activation(e_e[:], z_e[:], ACT.Exp).then_inc(exp_out, 1)
            roots(4)
            for q, (c0, cw) in enumerate(GROUPS):
                act.wait_ge(elu_in, NQ + q + 1)
                nc.scalar.activation(tmp2[:, 0:cw], tmp[:, 0:cw], ACT.Exp).then_inc(elu_exp, 1)
            roots(5)

        @block.vector
        def _(dve):
            chain = [0]

            def link(ins):
                chain[0] += 1
                ins.then_inc(dve_chain, 1)
                dve.wait_ge(dve_chain, chain[0])

            def scatter(name, values, key, gather):
                p = PASSES.index(name)
                with dve.Fori(0, EC // 2) as i:
                    for s in range(2):
                        dve.wait_ge(chunk_done, (EC + 2) * p + i * 2 + s + 1)
                        nc.vector.tensor_scalar(onehot[s][:], node_iota[:], key[:, bass.ds(i * 2 + s, 1)], None,
                                                ALU.is_equal)
                        if gather:
                            dve.wait_ge(gathered[s], 16 * (EC // 2 * GATHERS.index(name)) + i * 16 + 16)
                        nc.vector.tensor_scalar(msg[s][:], rows[s][:] if gather else ones[0:P, :],
                                                values[:, bass.ds(i * 2 + s, 1)], None, ALU.mult
                                                ).then_inc(msg_ready, 1)

            def sums(name, to):
                p = PASSES.index(name)
                for q, (c0, cw) in enumerate(GROUPS):
                    dve.wait_ge(scatter_done, NQ * p + q + 1)
                    to(q, c0, cw).then_inc(agg_out, 1)

            def mean(q, c0, cw):
                return nc.vector.tensor_tensor(aggT[:, c0:c0 + cw], acc[:, q, 0:cw], normT[:, c0:c0 + cw], ALU.mult)

            def layer_norm(name, n, to):
                for q in range(NQ):
                    dve.wait_ge(mm_done, filled(name, q))
                    for j, b in enumerate(BLOCKS[q]):
                        last = nc.vector.bn_stats(stats[:, b, :], acc[0:P, q, j * D:(j + 1) * D])
                link(last)
                for b in range(H):
                    last = nc.vector.bn_aggr(mv[:, b, :], stats[:, b, :])
                last.then_inc(var_ready, 1)
                dve.wait_ge(std_ready, n)
                link(nc.vector.reciprocal(rstd[:], rstd[:]))
                for q in range(NQ):
                    for j, b in enumerate(BLOCKS[q]):
                        last = nc.vector.tensor_scalar(to[:, b, :], acc[0:P, q, j * D:(j + 1) * D], mv[:, b, 0:1],
                                                       rstd[:, b:b + 1], ALU.subtract, ALU.mult)
                    last.then_inc(ev_dve, 1)
                dve.wait_ge(*emptied(name, NQ - 1))

            def copies(name, to):
                for q, (c0, cw) in enumerate(GROUPS):
                    dve.wait_ge(mm_done, filled(name, q))
                    nc.vector.tensor_copy(to[:, c0:c0 + cw], acc[:, q, 0:cw]).then_inc(ev_dve, 1)
                dve.wait_ge(*emptied(name, NQ - 1))

            def add_x(name, bias):
                for q, (c0, cw) in enumerate(GROUPS):
                    dve.wait_ge(mm_done, filled(name, q))
                    nc.vector.scalar_tensor_tensor(out=yT[:, c0:c0 + cw], in0=acc[:, q, 0:cw], scalar=bias,
                                                   in1=xT[:, c0:c0 + cw], op0=ALU.add, op1=ALU.add).then_inc(ev_dve, 1)

            nc.vector.memset(ones[:], 1.0)
            nc.vector.memset(zeros[:], 0.0)
            nc.vector.memset(eps[:], LN_EPS)
            link(nc.vector.memset(ones_e[:], 1.0))
            dve.wait_ge(loaded, 16 * len(loads))
            dve.wait_ge(consts_ready, 3)
            nc.vector.tensor_copy(src_f[:], src_i[:])
            nc.vector.tensor_tensor(BS[:], BS[:], BN_[:], ALU.add)
            link(nc.vector.tensor_copy(dst_f[:], dst_i[:]))
            nc.vector.memset(tmp2[:, 0:1], 0.0).then_inc(edges_ready, 1)
            copies("fwd0", xT)
            scatter("agg0", w_e, src_f, True)
            sums("agg0", lambda q, c0, cw: nc.vector.tensor_copy(aggT[:, c0:c0 + cw], acc[:, q, 0:cw]))
            add_x("lin0", B0[:])
            layer_norm("back0", 1, x)
            link(nc.vector.memset(tmp2[:, 0:1], 0.0))
            nc.vector.memset(tmp2[:, 0:1], 0.0).then_inc(x_new, 1)
            copies("fwd1", xT)
            scatter("deg", ones_e, dst_f, False)
            sums("deg", lambda q, c0, cw: nc.vector.tensor_scalar(normT[:, c0:c0 + cw], acc[:, q, 0:cw], 1.0, None, ALU.max))
            dve.wait_ge(agg_out, 2 * NQ)
            link(nc.vector.reciprocal(normT[:], normT[:]))
            scatter("agg1", ones_e, dst_f, True)
            sums("agg1", mean)
            for q, (c0, cw) in enumerate(GROUPS):
                dve.wait_ge(*emptied("lin1", q))
                nc.vector.tensor_tensor(yT[:, c0:c0 + cw], yT[:, c0:c0 + cw], xT[:, c0:c0 + cw], ALU.add).then_inc(elu_in, 1)
            layer_norm("back1", 2, x)
            link(nc.vector.memset(tmp2[:, 0:1], 0.0))
            nc.vector.memset(tmp2[:, 0:1], 0.0).then_inc(x_new, 1)
            copies("fwd2", xT)
            scatter("agg2", ones_e, dst_f, True)
            sums("agg2", mean)
            add_x("l2o", BM2[:])
            layer_norm("back2", 3, x)
            link(nc.vector.memset(tmp2[:, 0:1], 0.0))
            nc.vector.memset(tmp2[:, 0:1], 0.0).then_inc(x_new, 1)
            copies("fwd3", xT)
            for q, (c0, cw) in enumerate(GROUPS):
                dve.wait_ge(mm_done, filled("h3", q))
                nc.vector.tensor_scalar(hidden[:, 0, c0:c0 + cw], acc[:, q, 0:cw], B3[:], None, ALU.add).then_inc(ev_dve, 1)
            for q in range(NQ):
                dve.wait_ge(mm_done, filled("s3", q))
                nb = len(BLOCKS[q])
                nc.vector.tensor_copy(s_node[:, q * QB:q * QB + nb, :].rearrange("p h k -> p (h k)"),
                                      acc[0:P, q, 0:2 * nb]).then_inc(ev_dve, 1)
            nc.vector.memset(tmp2[:, 0:1], 0.0).then_inc(scol_done, 2)
            for k in range(2):
                with dve.Fori(0, EC // 2) as i:
                    for s in range(2):
                        dve.wait_ge(sgathered[s], 16 * (EC // 2 * k) + i * 16 + 16)
                        nc.vector.tensor_copy(s_of[k][:, bass.ds(i * 2 + s, 1)], srow[s][:, 1 - k:2 - k]).then_inc(scol_done, 1)
            dve.wait_ge(scol_done, 2 * EC + 2)
            link(nc.vector.tensor_tensor(s_of[0][:], s_of[0][:], s_of[1][:], ALU.add))
            link(nc.vector.scalar_tensor_tensor(out=z_e[:], in0=s_of[0][:], scalar=ALPHA, in1=s_of[0][:],
                                                op0=ALU.mult, op1=ALU.max))
            nc.vector.tensor_reduce(pmax[:], z_e[:], AX_X, ALU.max).then_inc(max_in, 1)
            dve.wait_ge(max_out, 1)
            nc.vector.tensor_scalar(z_e[:], z_e[:], gmax[:], None, ALU.subtract).then_inc(exp_in, 1)
            dve.wait_ge(exp_out, 1)
            scatter("rowsum", e_e, src_f, False)
            sums("rowsum", lambda q, c0, cw: nc.vector.tensor_copy(normT[:, c0:c0 + cw], acc[:, q, 0:cw]))
            scatter("agg3", e_e, src_f, True)
            sums("agg3", lambda q, c0, cw: nc.vector.tensor_copy(aggT[:, c0:c0 + cw], acc[:, q, 0:cw]))
            for q, (c0, cw) in enumerate(GROUPS):
                c = slice(c0, c0 + cw)
                link(nc.vector.tensor_scalar(tmp[:, 0:cw], normT[:, c], SUM_EPS, None, ALU.add))
                link(nc.vector.reciprocal(tmp2[:, 0:cw], tmp[:, 0:cw]))
                dve.wait_ge(mm_done, filled("lin3", q))
                link(nc.vector.scalar_tensor_tensor(out=tmp[:, 0:cw], in0=normT[:, c], scalar=B3[:], in1=acc[:, q, 0:cw],
                                                    op0=ALU.mult, op1=ALU.add))
                link(nc.vector.tensor_tensor(tmp[:, 0:cw], tmp[:, 0:cw], tmp2[:, 0:cw], ALU.mult))
                nc.vector.tensor_tensor(yT[:, c], tmp[:, 0:cw], xT[:, c], ALU.add).then_inc(ev_dve, 1)
                dve.wait_ge(*emptied("lin3", q))
            layer_norm("back3", 4, x3)
            for q, (c0, cw) in enumerate(GROUPS):
                c = slice(c0, c0 + cw)
                dve.wait_ge(mm_done, filled("fwd3n", q))
                link(nc.vector.tensor_scalar(yT[:, c], acc[:, q, 0:cw], G3[:], BE3[:], ALU.mult, ALU.add))
                nc.vector.tensor_scalar(tmp[:, 0:cw], yT[:, c], 0.0, None, ALU.min).then_inc(elu_in, 1)
                dve.wait_ge(elu_exp, q + 1)
                link(nc.vector.scalar_tensor_tensor(out=tmp[:, 0:cw], in0=yT[:, c], scalar=0.0, in1=tmp2[:, 0:cw],
                                                    op0=ALU.max, op1=ALU.add))
                nc.vector.scalar_tensor_tensor(out=yT[:, c], in0=tmp[:, 0:cw], scalar=-1.0, in1=xT[:, c],
                                               op0=ALU.add, op1=ALU.add).then_inc(ev_dve, 1)
                dve.wait_ge(*emptied("fwd3n", q))
            layer_norm("back4", 5, x)
            link(nc.vector.memset(tmp2[:, 0:1], 0.0))
            nc.vector.memset(tmp2[:, 0:1], 0.0).then_inc(x_new, 1)


_INS = ["x", "src", "dst", "edge_weight", "L0_gnn_weight", "L0_gnn_bias", "L1_gnn_W_self", "L1_gnn_b_self",
        "L1_gnn_W_nei", "L1_gnn_b_nei", "L2_gnn_W_l", "L2_gnn_b_l", "L2_gnn_W_r", "L2_gnn_Wm1", "L2_gnn_bm1",
        "L2_gnn_Wm2", "L2_gnn_bm2", "L3_gnn_W", "L3_gnn_a", "L3_gnn_bias", "L3_gnn_gamma", "L3_gnn_beta"]
_TRANSPOSED = ("L1_gnn_W_self", "L1_gnn_W_nei")


def kernel(**inputs):
    import numpy as np
    import concourse.bacc as bacc
    from concourse.bass_utils import run_bass_kernel_spmd

    nc = bacc.Bacc("TRN2", target_bir_lowering=False, num_devices=1)
    arrays, args = {}, []
    for name in _INS:
        a = np.asarray(inputs[name])
        a = np.ascontiguousarray(a.T if name in _TRANSPOSED else a)
        arrays[f"in_{name}"] = a
        args.append(nc.dram_tensor(f"in_{name}", a.shape, mybir.dt.from_np(a.dtype), kind="ExternalInput").ap())
    out = nc.dram_tensor("out_x", inputs["x"].shape, F32, kind="ExternalOutput").ap()
    gnn_stack(nc, *args, out)
    r = run_bass_kernel_spmd(nc, [arrays], core_ids=[0])
    return r.results[0]["out_x"]
```

```python
from contextlib import ExitStack, contextmanager

import concourse.bass as bass
from concourse import mybir

ALU = mybir.AluOpType
ACT = mybir.ActivationFunctionType
AX_X = mybir.AxisListType.X
F32 = mybir.dt.float32
F16 = mybir.dt.float16
F8 = mybir.dt.float8e4
U8 = mybir.dt.uint8
I32 = mybir.dt.int32
RMAX = bass.bass_isa.ReduceOp.max

LN_EPS = 1e-5
ALPHA = 0.2
SUM_EPS = 1e-8
BIG = 1e30
F16_MAX = 65504.0
ROUND = 1.5 * 2.0 ** 23


def gnn_stack(nc, x_in, src, dst, edge_weight, w0, b0, w_selfT, b_self, w_neiT, b_nei,
              w_l, b_l, w_r, wm1, bm1, wm2, bm2, w3, a3, b3, gamma, beta, out):
    N, D = x_in.shape
    E = src.shape[0]
    P = 125
    H = N // P
    EC = E // P
    QB = 4
    QW = QB * P
    GROUPS = [(q * QW, min(QW, N - q * QW)) for q in range(-(-N // QW))]
    NQ = len(GROUPS)
    BLOCKS = [list(range(q * QB, min(H, (q + 1) * QB))) for q in range(NQ)]
    HALVES = w_l.shape[1] // D
    GD = 5
    NG = N // GD
    GT = NG // P
    ROWE = 32
    WIN = 256
    WC = WIN // 128
    NROW = (E - WIN) // ROWE + 1
    UG = 5
    UC = UG * WC
    KW = H * GD
    UNITS = P // (UG * GD)
    KEY0 = 1000.0
    CS = 16.0
    WS_ = 8192.0
    XS = 1024.0
    assert H * P == N and EC * P == E and EC % 2 == 0 and D == 128 and E % ROWE == 0
    assert GT * P == NG and UNITS * UG * GD == P and H % 2 == 1

    with ExitStack() as ctx:
        def sb(name, shape, dt=F32):
            return ctx.enter_context(nc.sbuf_tensor(name, shape, dt))

        def sem(name):
            return ctx.enter_context(nc.semaphore(name))

        acc = ctx.enter_context(nc.psum_tensor("acc", [128, 8, 512], F32))

        x = sb("x", [P, H, D])
        xT = sb("xT", [128, N])
        aggT = sb("aggT", [128, N])
        normT = sb("normT", [128, N])
        yT = sb("yT", [128, N])
        hidden = sb("hidden", [128, HALVES, N])
        x3 = sb("x3", [P, H, D])
        hid2 = [aggT, yT]
        src_i = sb("src_i", [P, EC], I32)
        dst_i = sb("dst_i", [P, EC], I32)
        w_e = sb("w_e", [P, EC])
        ident = sb("ident", [128, 128])
        ident16 = sb("ident16", [128, 128], F16)
        ones = sb("ones", [128, 128])
        ones16 = sb("ones16", [128, 128], F16)
        eps = sb("eps", [128, 1])
        W0, WS, WN, W3 = sb("W0", [D, D]), sb("WS", [D, D]), sb("WN", [D, D]), sb("W3", [D, D])
        WL, WR = sb("WL", [D, HALVES * D]), sb("WR", [D, HALVES * D])
        WM1 = sb("WM1", [D, HALVES, HALVES * D])
        WM2 = sb("WM2", [D, HALVES, D])
        A3 = sb("A3", [D, 2])
        A3S = sb("A3S", [D, 128])
        B0, BS, BN_, B3, G3, BE3, BM2 = (sb(n, [D, 1]) for n in ("B0", "BS", "BN", "B3", "G3", "BE3", "BM2"))
        BL, BM1 = sb("BL", [D, HALVES]), sb("BM1", [D, HALVES])
        stats = sb("stats", [P, H, 6])
        mv = sb("mv", [P, H, 2])
        rstd = sb("rstd", [P, H])
        s_node = sb("s_node", [P, H, 2])
        small = sb("small", [128, 64])
        sb_fast0 = sb("sb_fast0", [128, 1])
        tmp = sb("tmp", [128, QW])
        tmp2 = sb("tmp2", [128, QW])
        flag_i = sb("flag_i", [128, 2], I32)
        FAST0, FAST = 0, 1

        ARENA = 85 * 1024
        arena = sb("arena", [128, ARENA], U8)
        at = [0]

        def tile(shape, dt=F32):
            size = {F32: 4, I32: 4, F16: 2, U8: 1}[dt]
            n = 1
            for d in shape[1:]:
                n *= d
            flat = arena[0:shape[0], at[0]:at[0] + n * size].bitcast(dt)
            at[0] += -(-n * size // 32) * 32
            assert at[0] <= ARENA, at[0]
            if len(shape) == 2:
                return flat
            names = "abc"[:len(shape) - 1]
            return flat.rearrange(f"p ({' '.join(names)}) -> p {' '.join(names)}",
                                  **{k: v for k, v in zip(names[1:], shape[2:])})

        keys = [tile([128, NG * WC], F16) for _ in range(4)]
        k_lo, k_key, k_wh, k_wl = keys
        iota_lo = tile([128, 128, UC], F16)
        iota_key = tile([128, KW, UC], F16)
        build_at = at[0]
        win_i = [tile([P, GT, WIN], I32) for _ in range(2)]
        win_w = tile([P, GT, WIN])
        cut = [tile([P, GT, WIN]) for _ in range(6)]
        diag = hidden[0:P, 0, :]
        frow = hidden[0:P, 1, :]
        thr = tile([P, GT])
        start_i = tile([P, GT], I32)
        at[0] = build_at
        hot = [[tile([128, 128, UC], F16), tile([128, KW, UC], F16), tile([128, 128, UC], F16), tile([128, 128, UC], F16)]
               for _ in range(2)]
        c_stage = [tile([128, H, P], U8) for _ in range(2)]
        strip = [tile([P, H, P]), x3[:, :, 0:P]]
        wblk = [tile([P, QW]) for _ in range(2)]
        xb = [tile([P, D]) for _ in range(2)]
        at[0] = 0
        cb = [tile([128, QB, N], U8) for _ in range(2)]
        x16 = [tile([P, H, D], F16) for _ in range(2)]
        at[0] = 0
        SWEEPS = [([[0, 1, 2, 3], [4, 5, 6, 7], [8, 9, 10, 11], [12, 13, 14]], 5, 2),
                  ([[15, 16, 17, 18], [19, 20, 21, 22], [23, 24]], 4, 3)]
        SWW = max(sum(map(len, g)) for g, _, _ in SWEEPS) * P
        c3 = [tile([128, H, P], U8) for _ in range(2)]
        relu3 = tile([P, SWW])
        t3 = [tile([P, SWW]) for _ in range(2)]
        hN = tile([P, H, D + 2])
        raw3 = tile([P, H, D + 1])
        e3 = [tile([P, QW]) for _ in range(4)]
        mask3 = [tile([P, QW], F16) for _ in range(4)]
        rmax = [tile([P, 4]) for _ in range(2)]
        mx = tile([P, H, 8])
        junk = tile([P, QW])
        zero3 = tile([P, 3 * (D + 1)])
        arow = hidden[0:P, 1, :]
        apos = normT[0:P, :]
        sd = small[0:P, 32:32 + H]
        bj = x3[:, 0, 0:H]

        at[0] = 0
        node_iota = tile([P, N])
        onehot = [tile([P, N]) for _ in range(2)]
        src_f, dst_f, ones_e, z_e, e_e = (tile([P, EC]) for _ in range(5))
        s_of = [tile([P, EC]) for _ in range(2)]
        zeros = tile([P, QW])
        gidx = [tile([P, 1], I32) for _ in range(2)]
        rows_g = [tile([P, D]) for _ in range(2)]
        srow = [tile([P, 2]) for _ in range(2)]
        msg = [tile([P, D]) for _ in range(2)]
        pause = tile([P, 1])
        tables = [x_in] + [nc.dram_tensor(f"x{n}_table", [N, D], F32, kind="Internal").ap() for n in (1, 2, 3)]
        s_table = nc.dram_tensor("s_table", [N, 2], F32, kind="Internal").ap()
        PASSES = ["agg0", "deg", "agg1", "agg2", "rowsum", "agg3"]

        c_dram = nc.dram_tensor("counts", [H, 128, N], U8, kind="Internal").ap()
        wide = [nc.dram_tensor(f"wide{k}", [NROW, WIN], dt, kind="Internal").ap() for k, dt in enumerate((I32, I32, F32))]

        loaded = sem("loaded")
        edges_loaded = sem("edges_loaded")
        wide_ready = sem("wide_ready")
        consts_ready = sem("consts_ready")
        dve_chain = sem("dve_chain")
        branch_chain = {(which, yes): sem(f"dve_chain_{which}_{yes}") for which in (FAST0, FAST) for yes in (True, False)}
        first_ready = sem("first_ready")
        first_mm = sem("first_mm")
        first_out = sem("first_out")
        starts_ready = sem("starts_ready")
        windows_in = sem("windows_in")
        cut_ready = sem("cut_ready")
        turned = sem("turned")
        turned_out = sem("turned_out")
        hot_ready = sem("hot_ready")
        lo_ready = sem("lo_ready")
        row_done = sem("row_done")
        x3_ready = sem("x3_ready")
        unit_mm = sem("unit_mm")
        unit_out = sem("unit_out")
        c_stored = [sem(f"c_stored{k}") for k in range(2)]
        xb_loaded = [sem(f"xb_loaded{k}") for k in range(2)]
        wt_done = sem("wt_done")
        wblk_ready = sem("wblk_ready")
        prod_done = sem("prod_done")
        prod_added = sem("prod_added")
        x16_ready = sem("x16_ready")
        cb_loaded = [sem(f"cb_loaded{k}") for k in range(2)]
        dense_mm = sem("dense_mm")
        dense_out = sem("dense_out")
        mm_done = sem("mm_done")
        ev_dve = sem("ev_dve")
        ev_act = sem("ev_act")
        var_ready = sem("var_ready")
        std_ready = sem("std_ready")
        elu_in = sem("elu_in")
        elu_exp = sem("elu_exp")
        y1_ready = sem("y1_ready")
        x_new = sem("x_new")
        max_in = sem("max_in")
        max_out = sem("max_out")
        l3_ready = sem("l3_ready")
        c3_loaded = [sem(f"c3_loaded{k}") for k in range(2)]
        c3_mm = sem("c3_mm")
        relu_ready = sem("relu_ready")
        relu_used = sem("relu_used")
        t3_ready = sem("t3_ready")
        mask_ready = sem("mask_ready")
        mask_used = sem("mask_used")
        e3_ready = sem("e3_ready")
        e3_used = sem("e3_used")
        sweep_done = sem("sweep_done")
        sweep_out = sem("sweep_out")
        eps_in = sem("eps_in")
        eps_out = sem("eps_out")
        out_stored = sem("out_stored")
        flag_sums = sem("flag_sums")
        flag_mm = sem("flag_mm")
        fast0_ready = sem("fast0_ready")
        fast_ready = sem("fast_ready")
        sums_ready = sem("sums_ready")
        STAGES = ("layer0", "layers12", "layer3")
        prepared = {p: sem(f"prepared_{p}") for p in STAGES}
        node_iota_ready = {p: sem(f"node_iota_ready_{p}") for p in STAGES}
        table_ready = [sem(f"table_ready{n}") for n in range(4)]
        s_table_ready = sem("s_table_ready")
        gidx_ready = {p: sem(f"gidx_ready_{p}") for p in ("agg0", "agg1", "agg2", "agg3", "s0", "s1")}
        gathered = {p: [sem(f"gathered_{p}_{k}") for k in range(2)] for p in gidx_ready}
        msg_ready = {p: sem(f"msg_ready_{p}") for p in PASSES}
        chunk_done = {p: sem(f"chunk_done_{p}") for p in PASSES}
        scatter_done = {p: sem(f"scatter_done_{p}") for p in PASSES}
        scatter_out = {p: sem(f"scatter_out_{p}") for p in PASSES}
        s_col_done = sem("s_col_done")
        general_max = sem("general_max")
        general_gmax = sem("general_gmax")
        logits_in = sem("logits_in")
        logits_out = sem("logits_out")
        lin3_done = sem("lin3_done")
        y3_ready = sem("y3_ready")
        back3_done = sem("back3_done")

        ROUNDS = [("fwd0", ev_dve),
                  ("lin0", ev_dve), ("back0", ev_dve), ("fwd1", ev_dve),
                  ("lin1", ev_act), ("back1", ev_dve), ("fwd2", ev_dve),
                  ("l2h0", ev_act), ("l2h1", ev_act), ("l2m0", ev_act), ("l2m1", ev_act), ("l2o", ev_dve),
                  ("back2", ev_dve), ("fwd3", ev_dve),
                  ("h3", ev_dve), ("s3", ev_dve), ("arow", ev_act), ("hnode", ev_dve),
                  ("fwd3n", ev_dve), ("back4", ev_dve)]
        NUMBER = {name: n for n, (name, _) in enumerate(ROUNDS)}

        def filled(name, q):
            return NQ * NUMBER[name] + q + 1

        def emptied(name, q):
            n = NUMBER[name]
            same = sum(1 for _, s in ROUNDS[:n] if s is ROUNDS[n][1])
            return ROUNDS[n][1], NQ * same + q + 1

        def takes(eng, which):
            eng.wait_ge(fast0_ready if which == FAST0 else fast_ready, 1)
            return eng.value_load(flag_i[0:1, which:which + 1], min_val=0, max_val=1)

        def wait(eng, s, value):
            if not isinstance(value, int) or value > 0:
                eng.wait_ge(s, value)

        SLOTS = {2: 0, 5: 1, 9: 2, 12: 3, 16: 4, 19: 5, 23: 6}
        SLOT_UNIT = {k: g // UG for g, k in SLOTS.items()}
        P_UNIT = {k: SLOT_UNIT[k + 1] if k + 1 < NQ else UNITS - 1 for k in range(NQ)}

        loads = [(x[:], x_in.rearrange("(h p) d -> p h d", p=P)),
                 (W0[:], w0), (WS[:], w_selfT), (WN[:], w_neiT), (W3[:], w3), (WL[:], w_l), (WR[:], w_r),
                 (WM1[:], wm1.rearrange("(k p) n -> p k n", p=D)),
                 (WM2[:], wm2.rearrange("(k p) n -> p k n", p=D)),
                 (A3[:], a3.rearrange("(k p) -> p k", p=D)),
                 (BL[:], b_l.rearrange("(k p) -> p k", p=D)),
                 (BM1[:], bm1.rearrange("(k p) -> p k", p=D)),
                 ] + [(t[:], v.rearrange("(p k) -> p k", k=1)) for t, v in
                      ((B0, b0), (BS, b_self), (BN_, b_nei), (B3, b3), (G3, gamma), (BE3, beta), (BM2, bm2))]

        def block_pairs(eng, body):
            body(0, 0, True)
            body(1, 1, True)
            body(2, 0, True)
            with eng.Fori(1, (H - 1) // 2 - 1) as i:
                body(i * 2 + 1, 1, True)
                body(i * 2 + 2, 0, True)
            body(H - 2, 1, True)
            body(H - 1, 0, False)

        block = ctx.enter_context(nc.Block())

        @block.sync
        def _(sp):
            for to, frm in ((dst_i, dst), (src_i, src), (w_e, edge_weight)):
                sp.dma_start(to[:], frm.rearrange("(p c) -> p c", p=P)).then_inc(edges_loaded, 16)
            rows16 = NROW // 16 * 16
            for to, frm in zip(wide, (src, dst, edge_weight)):
                for r0, nr in ((0, rows16), (rows16, NROW - rows16)):
                    over = bass.AP(frm.tensor, r0 * ROWE, [[ROWE, nr], [1, WIN]])
                    sp.dma_start(to[r0:r0 + nr, :], over).then_inc(wide_ready, 16)
            with nc.allow_non_contiguous_dma(reason="a bias per feature: 128 short runs each"):
                for to, frm in loads:
                    sp.dma_start(to, frm).then_inc(loaded, 16)

            fast0 = takes(sp, FAST0)
            with sp.If(fast0 > 0):
                sp.wait_ge(turned_out, 4 * GT)
                def body(b, par, more):
                    wait(sp, prod_done, 1 + NQ * (b - 1) if not isinstance(b, int) or b > 1 else 0)
                    sp.wait_ge(unit_out, UNITS * (b + 1))
                    sp.dma_start(xb[par][:], x_in[bass.ds(b * P, P), :]).then_inc(xb_loaded[par], 16)
                    sp.dma_start(c_dram[bass.ds(b, 1)].rearrange("a p f -> p (a f)"),
                                 c_stage[par].rearrange("p a b -> p (a b)")).then_inc(c_stored[par], 16)
                block_pairs(sp, body)
                sp.wait_ge(c_stored[0], 16 * (H // 2 + 1))
                sp.wait_ge(c_stored[1], 16 * (H // 2))
                sp.wait_ge(prod_added, NQ + NQ * H)

            def load_counts(layer):
                for q, (c0, cw) in enumerate(GROUPS):
                    n = NQ * layer + q
                    wait(sp, dense_mm, n - 1)
                    nb = len(BLOCKS[q])
                    sp.dma_start(cb[n % 2][:, 0:nb, :],
                                 c_dram[q * QB:q * QB + nb].rearrange("b p f -> p b f")).then_inc(cb_loaded[n % 2], 16)

            def store_table(layer):
                sp.wait_ge(x_new, layer)
                sp.dma_start(tables[layer].rearrange("(h p) d -> p h d", p=P), x[:]).then_inc(table_ready[layer], 16)
                sp.wait_ge(table_ready[layer], 16)

            with sp.If(fast0 > 0):
                load_counts(0)
            fast = takes(sp, FAST)
            with sp.If(fast > 0):
                load_counts(1)
                sp.wait_ge(dense_mm, 2 * NQ)
                for w, (groups, _, _) in enumerate(SWEEPS):
                    g0 = H * sum(len(g) for g, _, _ in SWEEPS[:w])

                    def body(b, par, more, w=w, g0=g0, ng=len(groups)):
                        if w == 0:
                            wait(sp, c3_mm, ng * (b - 1) if not isinstance(b, int) or b > 1 else 0)
                        else:
                            wait(sp, c3_mm, g0 + ng * (b - 1) if not isinstance(b, int) or b > 1 else g0)
                        sp.dma_start(c3[par].rearrange("p a b -> p (a b)"),
                                     c_dram[bass.ds(b, 1)].rearrange("a p f -> p (a f)")).then_inc(c3_loaded[par], 16)
                    block_pairs(sp, body)
            with sp.If(fast < 1):
                for layer in (1, 2, 3):
                    store_table(layer)
                sp.wait_ge(l3_ready, 1)
                sp.dma_start(s_table.rearrange("(h p) k -> p h k", p=P), s_node[:]).then_inc(s_table_ready, 16)
                sp.wait_ge(s_table_ready, 16)
            sp.wait_ge(x_new, 4)
            sp.dma_start(out.rearrange("(h p) d -> p h d", p=P), x[:]).then_inc(out_stored, 16)
            sp.wait_ge(out_stored, 16)

        @block.gpsimd
        def _(pool):
            nc.gpsimd.memset(ident[:], 0.0).then_inc(consts_ready, 1)
            pool.wait_ge(consts_ready, 1)
            nc.gpsimd.affine_select(out=ident[:], in_=ident[:], compare_op=ALU.not_equal, fill=1.0, base=0,
                                    pattern=[[-1, 128]], channel_multiplier=1)
            nc.gpsimd.iota(thr, [[GD * P, GT]], base=0, channel_multiplier=GD,
                           allow_small_or_imprecise_dtypes=True).then_inc(consts_ready, 1)
            nc.gpsimd.iota(iota_lo, [[1, 128], [0, UC]], base=0, channel_multiplier=0,
                           allow_small_or_imprecise_dtypes=True)
            nc.gpsimd.iota(iota_key, [[1, KW], [0, UC]], base=int(KEY0), channel_multiplier=0,
                           allow_small_or_imprecise_dtypes=True).then_inc(consts_ready, 1)
            pool.wait_ge(wide_ready, 16 * 6)
            pool.wait_ge(starts_ready, 1)
            for t in range(GT):
                for to, frm in zip((win_i[0], win_i[1], win_w), wide):
                    nc.gpsimd.indirect_dma_start(out=to[:, t, :], out_offset=None, in_=frm,
                                                 in_offset=bass.IndirectOffsetOnAxis(start_i[:, t:t + 1], 0)
                                                 ).then_inc(windows_in, 16)

            def gather(name, idx, table, to, free, first):
                with pool.Fori(0, EC // 2) as i:
                    for k in range(2):
                        pool.wait_ge(free, i * 2 + (first + k + 1))
                        nc.gpsimd.tensor_copy(gidx[k], idx[:, bass.ds(i * 2 + k, 1)]).then_inc(gidx_ready[name], 1)
                        pool.wait_ge(gidx_ready[name], i * 2 + (k + 1))
                        nc.gpsimd.tensor_tensor(pause, ident[0:P, 0:1], ident[0:P, 0:1], ALU.add)
                        nc.gpsimd.indirect_dma_start(out=to[k], out_offset=None, in_=table,
                                                     in_offset=bass.IndirectOffsetOnAxis(gidx[k][:, 0:1], 0)
                                                     ).then_inc(gathered[name][k], 16)

            def node_indices(stage):
                nc.gpsimd.iota(node_iota, [[1, N]], base=0, channel_multiplier=0,
                               allow_small_or_imprecise_dtypes=True).then_inc(node_iota_ready[stage], 1)

            fast0 = takes(pool, FAST0)
            with pool.If(fast0 < 1):
                node_indices("layer0")
                gather("agg0", dst_i, tables[0], rows_g, chunk_done["agg0"], 0)
            fast = takes(pool, FAST)
            with pool.If(fast < 1):
                node_indices("layers12")
                for layer in (1, 2):
                    pool.wait_ge(table_ready[layer], 16)
                    gather(f"agg{layer}", src_i, tables[layer], rows_g, chunk_done[f"agg{layer}"], 0)
            pool.wait_ge(max_in, 1)
            nc.gpsimd.partition_all_reduce(small[0:P, 1:2], small[0:P, 0:1], P, RMAX).then_inc(max_out, 1)
            with pool.If(fast > 0):
                pool.wait_ge(max_in, 2)
                nc.gpsimd.partition_all_reduce(small[0:P, 3:4], small[0:P, 2:3], P, RMAX).then_inc(max_out, 1)
            with pool.If(fast < 1):
                pool.wait_ge(l3_ready, 1)
                node_indices("layer3")
                pool.wait_ge(s_table_ready, 16)
                for k, idx in enumerate((dst_i, src_i)):
                    gather(f"s{k}", idx, s_table, srow, s_col_done, EC * k)
                pool.wait_ge(general_max, 1)
                nc.gpsimd.partition_all_reduce(small[0:P, 23:24], small[0:P, 22:23], P, RMAX).then_inc(general_gmax, 1)
                pool.wait_ge(table_ready[3], 16)
                gather("agg3", dst_i, tables[3], rows_g, chunk_done["agg3"], 0)

        @block.tensor
        def _(pe):
            def fill(name, steps):
                before = ROUNDS[NUMBER[name] - 1][0] if NUMBER[name] else None
                for q, (c0, cw) in enumerate(GROUPS):
                    if before:
                        pe.wait_ge(*emptied(before, q))
                    steps(q, c0, cw).then_inc(mm_done, 1)

            def to_nodes(name, frm):
                def steps(q, c0, cw):
                    for j, b in enumerate(BLOCKS[q]):
                        last = nc.tensor.transpose(acc[0:P, q, j * D:(j + 1) * D], frm[:, b * P:(b + 1) * P], ident[:])
                    return last
                fill(name, steps)

            def to_features(name, frm):
                def steps(q, c0, cw):
                    for j, b in enumerate(BLOCKS[q]):
                        last = nc.tensor.transpose(acc[:, q, j * P:(j + 1) * P], frm[:, b, :], ident[0:P, 0:P])
                    return last
                fill(name, steps)

            def linear(name, terms):
                def steps(q, c0, cw):
                    for n, (w, v) in enumerate(terms):
                        last = nc.tensor.matmul(acc[:, q, 0:cw], w, v[:, c0:c0 + cw],
                                                start=(n == 0), stop=(n == len(terms) - 1))
                    return last
                fill(name, steps)

            def dense_sums(layer):
                pe.wait_ge(x16_ready, layer + 1)
                for q, (c0, cw) in enumerate(GROUPS):
                    n = NQ * layer + q
                    nb = len(BLOCKS[q])
                    pe.wait_ge(cb_loaded[n % 2], 16 * (n // 2 + 1))
                    wait(pe, dense_out, n - 1)
                    for h in range(H):
                        rhs = cb[n % 2].bitcast(F8)[0:P, 0:nb, h * P:(h + 1) * P]
                        for part in range(2):
                            last = nc.tensor.matmul(acc[:, n % 2, 0:cw], x16[part][:, h, :], rhs,
                                                    start=(h == 0 and part == 0), stop=(h == H - 1 and part == 1))
                        if layer == 0:
                            last = nc.tensor.matmul(acc[:, 2 + n % 2, 0:cw], ones16[0:P, :], rhs,
                                                    start=(h == 0), stop=(h == H - 1))
                    last.then_inc(dense_mm, 1)

            def scatter(name):
                for q, (c0, cw) in enumerate(GROUPS):
                    last = nc.tensor.matmul(acc[:, q, 0:cw], zeros[:, 0:D], zeros[:, 0:cw], start=True, stop=False)
                last.then_inc(chunk_done[name], 2)
                with pe.Fori(0, EC // 2) as i:
                    for k in range(2):
                        pe.wait_ge(msg_ready[name], i * 2 + (k + 1))
                        for q, (c0, cw) in enumerate(GROUPS):
                            last = nc.tensor.matmul(acc[:, q, 0:cw], msg[k], onehot[k][:, c0:c0 + cw],
                                                    start=False, stop=False)
                        last.then_inc(chunk_done[name], 1)
                for q, (c0, cw) in enumerate(GROUPS):
                    nc.tensor.matmul(acc[:, q, 0:cw], zeros[:, 0:D], zeros[:, 0:cw],
                                     start=False, stop=True).then_inc(scatter_done[name], 1)

            pe.wait_ge(first_ready, 1)
            for q, (c0, cw) in enumerate(GROUPS):
                nc.tensor.matmul(acc[0:P, q, 0:cw], ones[0:P, 0:P], diag[:, c0:c0 + cw],
                                 start=True, stop=True).then_inc(first_mm, 1)
            pe.wait_ge(cut_ready, 1)
            pe.wait_ge(first_out, NQ)
            n = 0
            for t in range(GT):
                for k, v in enumerate((cut[0], cut[1], cut[2], cut[3])):
                    wait(pe, turned_out, n - 7)
                    for h in range(WC):
                        last = nc.tensor.transpose(acc[:, n % 8, h * P:(h + 1) * P], v[:, t, h * 128:(h + 1) * 128],
                                                   ident[0:P, 0:P])
                    last.then_inc(turned, 1)
                    n += 1
            pe.wait_ge(turned_out, n)
            pe.wait_ge(flag_sums, 1)
            nc.tensor.matmul(acc[:, 0, 0:2], ones[0:P, :], small[0:P, 16:18], start=True, stop=True).then_inc(flag_mm, 1)
            fast0 = takes(pe, FAST0)

            def turn_step(k, par, bb):
                m = NQ * bb + k
                pe.wait_ge(unit_out, UNITS * (bb + 1))
                wait(pe, wblk_ready, m)
                for j, h in enumerate(BLOCKS[k]):
                    last = nc.tensor.transpose(acc[0:P, 6, j * P:(j + 1) * P], strip[par][:, h, :], ident[0:P, 0:P])
                last.then_inc(wt_done, 1)

            def product_step(k, par, bb):
                m = NQ * bb + k
                c0, cw = GROUPS[k]
                if k == 0:
                    pe.wait_ge(xb_loaded[par], bb // 2 * 16 + 16 if isinstance(bb, int) else (bb - par) * 8 + 16)
                pe.wait_ge(wblk_ready, m + 1)
                pe.wait_ge(prod_added, NQ + m)
                nc.tensor.matmul(acc[:, 7, 0:cw], xb[par][:], wblk[(par + k) % 2][:, 0:cw],
                                 start=True, stop=True).then_inc(prod_done, 1)

            def body(b, par, more):
                for g in range(UNITS * UG):
                    u, j = divmod(g, UG)
                    up = (par + u) % 2
                    if j == 0:
                        U = b * UNITS + u
                        pe.wait_ge(hot_ready, U + 1)
                        wait(pe, unit_out, U - 1)
                    lo, key, loh, lol = hot[up]
                    cbank = acc[:, 3 * up, j * KW:(j + 1) * KW] if j < 4 else acc[:, 3 * up + 2, 0:KW]
                    wbank = acc[:, 3 * up + 1, j * KW:(j + 1) * KW] if j < 4 else acc[:, 3 * up + 2, KW:2 * KW]
                    for c in range(WC):
                        cc = j * WC + c
                        nc.tensor.matmul(cbank, lo[:, :, cc], key[:, :, cc], start=(c == 0), stop=(c == WC - 1))
                    for c in range(WC):
                        cc = j * WC + c
                        nc.tensor.matmul(wbank, loh[:, :, cc], key[:, :, cc], start=(c == 0), stop=False)
                        last = nc.tensor.matmul(wbank, lol[:, :, cc], key[:, :, cc], start=False, stop=(c == WC - 1))
                    if j == UG - 1:
                        last.then_inc(unit_mm, 1)
                    if g in SLOTS and not (isinstance(b, int) and b == 0):
                        k = SLOTS[g]
                        if k:
                            product_step(k - 1, 1 - par, b - 1)
                        turn_step(k, 1 - par, b - 1)
                if not (isinstance(b, int) and b == 0):
                    product_step(NQ - 1, 1 - par, b - 1)
            with pe.If(fast0 > 0):
                block_pairs(pe, body)
                for k in range(NQ):
                    turn_step(k, 0, H - 1)
                    product_step(k, 0, H - 1)
            with pe.If(fast0 < 1):
                pe.wait_ge(prepared["layer0"], 1)
                scatter("agg0")

            pe.wait_ge(sums_ready, 1)
            pe.wait_ge(loaded, 16 * len(loads))
            to_features("fwd0", x)
            linear("lin0", [(W0[:], aggT)])
            to_nodes("back0", yT)
            to_features("fwd1", x)
            pe.wait_ge(*emptied("fwd1", NQ - 1))
            with pe.If(fast0 > 0):
                dense_sums(0)
            fast = takes(pe, FAST)
            with pe.If(fast < 1):
                pe.wait_ge(prepared["layers12"], 1)
                scatter("deg")
                pe.wait_ge(scatter_out["deg"], NQ)
                scatter("agg1")
            pe.wait_ge(sums_ready, 2)
            linear("lin1", [(WS[:], xT), (WN[:], aggT)])
            pe.wait_ge(y1_ready, NQ)
            to_nodes("back1", yT)
            to_features("fwd2", x)
            pe.wait_ge(*emptied("fwd2", NQ - 1))
            with pe.If(fast > 0):
                dense_sums(1)
            with pe.If(fast < 1):
                scatter("agg2")
            pe.wait_ge(sums_ready, 3)
            for k in range(HALVES):
                c = slice(k * D, (k + 1) * D)
                linear(f"l2h{k}", [(WL[:, c], aggT), (WR[:, c], xT)])
            for k in range(HALVES):
                c = slice(k * D, (k + 1) * D)
                linear(f"l2m{k}", [(WM1[:, j, c], hidden[:, j]) for j in range(HALVES)])
            linear("l2o", [(WM2[:, j, :], hid2[j]) for j in range(HALVES)])
            to_nodes("back2", yT)
            to_features("fwd3", x)
            linear("h3", [(W3[:], xT)])

            def node_terms(q, c0, cw):
                for j, b in enumerate(BLOCKS[q]):
                    last = nc.tensor.matmul(acc[0:P, q, 2 * j:2 * j + 2], hidden[:, 0, b * P:(b + 1) * P], A3[:],
                                            start=True, stop=True)
                return last
            fill("s3", node_terms)
            linear("arow", [(A3S[:], hidden[:, 0])])
            to_nodes("hnode", hidden[:, 0])
            pe.wait_ge(l3_ready, 1)
            with pe.If(fast > 0):
                for w, (groups, nacc, nct) in enumerate(SWEEPS):
                    g0 = H * sum(len(g) for g, _, _ in SWEEPS[:w])
                    ng = len(groups)
                    first_block = groups[0][0]
                    nblk = sum(map(len, groups))
                    if w:
                        pe.wait_ge(sweep_out, w)
                    for a in range(nacc):
                        m = min(3, nblk - 3 * a) * (D + 1)
                        nc.tensor.matmul(acc[0:P, a, 0:m], zero3[0:P, 0:P], zero3[0:P, 0:m], start=True, stop=False)

                    def may_count(b, par, k, w=w, g0=g0, ng=ng, nct=nct):
                        n = b * ng + (g0 + k)
                        older = n - nct + 1 if not isinstance(n, int) or b or k >= nct else g0
                        before = 16 * (H // 2 + 1 if par == 0 else H // 2) * w
                        if k == 0:
                            pe.wait_ge(c3_loaded[par], (b // 2 * 16 if isinstance(b, int) else (b - par) * 8) + (16 + before))
                        wait(pe, e3_ready, older)
                        wait(pe, mask_ready, older)

                    def counts(par, k, groups=groups, nacc=nacc, nct=nct):
                        for j, s in enumerate(groups[k]):
                            last = nc.tensor.matmul(acc[0:P, nacc + k % nct, j * P:(j + 1) * P],
                                                    c3[par].bitcast(F8)[0:P, s, :], ident16[0:P, 0:P], start=True, stop=True)
                        last.then_inc(c3_mm, 1)

                    def sums(b, par, k, g0=g0, ng=ng, groups=groups, first_block=first_block):
                        pe.wait_ge(e3_ready, b * ng + (g0 + k + 1))
                        for j, s in enumerate(groups[k]):
                            a, o = divmod(s - first_block, 3)
                            last = nc.tensor.matmul(acc[0:P, a, o * (D + 1):(o + 1) * (D + 1)], e3[k][:, j * P:(j + 1) * P],
                                                    hN[:, bass.ds(b, 1), 0:D + 1].rearrange("p a d -> p (a d)"),
                                                    start=False, stop=False, skip_group_check=True)
                        last.then_inc(e3_used, 1)

                    def body(b, par, more, ng=ng, counts=counts, may_count=may_count, sums=sums):
                        for k in range(ng):
                            nxt = (b, par, k + 2) if k + 2 < ng else (b + 1, 1 - par, k + 2 - ng) if more else None
                            if nxt:
                                may_count(*nxt)
                            sums(b, par, k)
                            if nxt:
                                counts(nxt[1], nxt[2])
                    for k in range(2):
                        may_count(0, 0, k)
                        counts(0, k)
                    block_pairs(pe, body)
                    for a in range(nacc):
                        m = min(3, nblk - 3 * a) * (D + 1)
                        last = nc.tensor.matmul(acc[0:P, a, 0:m], zero3[0:P, 0:P], zero3[0:P, 0:m], start=False, stop=True)
                    last.then_inc(sweep_done, 1)
            with pe.If(fast < 1):
                pe.wait_ge(logits_out, 1)
                pe.wait_ge(prepared["layer3"], 1)
                scatter("rowsum")
                pe.wait_ge(scatter_out["rowsum"], NQ)
                scatter("agg3")
                for q, (c0, cw) in enumerate(GROUPS):
                    pe.wait_ge(scatter_out["agg3"], q + 1)
                    nc.tensor.matmul(acc[:, q, 0:cw], W3[:], aggT[:, c0:c0 + cw], start=True, stop=True).then_inc(lin3_done, 1)
                for q, (c0, cw) in enumerate(GROUPS):
                    pe.wait_ge(y3_ready, q + 1)
                    for j, b in enumerate(BLOCKS[q]):
                        last = nc.tensor.transpose(acc[0:P, q, j * D:(j + 1) * D], yT[:, b * P:(b + 1) * P], ident[:])
                    last.then_inc(back3_done, 1)
            pe.wait_ge(x3_ready, 1)
            to_features("fwd3n", x3)
            to_nodes("back4", yT)

        @block.scalar
        def _(act):
            def roots(n):
                act.wait_ge(var_ready, n)
                nc.scalar.activation(rstd[:], mv[:, :, 1], ACT.Sqrt, bias=eps[0:P, :]).then_inc(std_ready, 1)

            def relus(name, to, bias):
                for q, (c0, cw) in enumerate(GROUPS):
                    act.wait_ge(mm_done, filled(name, q))
                    nc.scalar.activation(to[:, c0:c0 + cw], acc[:, q, 0:cw], ACT.Relu, bias=bias).then_inc(ev_act, 1)

            for q, (c0, cw) in enumerate(GROUPS):
                act.wait_ge(first_mm, q + 1)
                nc.scalar.copy(frow[:, c0:c0 + cw], acc[0:P, q, 0:cw]).then_inc(first_out, 1)

            n = 0
            for t in range(GT):
                for k in range(4):
                    act.wait_ge(turned, n + 1)
                    nc.scalar.copy(keys[k][:, t * P * WC:(t + 1) * P * WC].rearrange("p (g h) -> p h g", h=WC),
                                   acc[:, n % 8, 0:WC * P].rearrange("p (h g) -> p h g", h=WC)).then_inc(turned_out, 1)
                    n += 1

            def turn_out(k, par, bb):
                m = NQ * bb + k
                c0, cw = GROUPS[k]
                act.wait_ge(wt_done, m + 1)
                wait(act, prod_done, m)
                nc.scalar.copy(wblk[(par + k) % 2][:, 0:cw], acc[0:P, 6, 0:cw]).then_inc(wblk_ready, 1)

            def body(b, par, more):
                for u in range(UNITS):
                    up = (par + u) % 2
                    if not (isinstance(b, int) and b == 0):
                        for k in range(NQ):
                            if SLOT_UNIT[k] == u:
                                turn_out(k, 1 - par, b - 1)
                    if u == 0 and not (isinstance(b, int) and b == 0):
                        wait(act, c_stored[par], b // 2 * 16 if isinstance(b, int) else (b - par) * 8)
                        wait(act, wt_done, NQ * (b - 1))
                    act.wait_ge(unit_mm, b * UNITS + u + 1)
                    for to, bank, scale, rows in ((strip[par], 1, 1.0 / WS_, P), (c_stage[par].bitcast(F8), 0, CS, 128)):
                        o = u * UG * GD
                        extra = {"saturate": False} if bank == 0 else {}
                        nc.scalar.activation(to[:, :, o:o + 4 * GD].rearrange("p h (j l) -> p h j l", j=4),
                                             acc[0:rows, 3 * up + bank, 0:4 * KW].rearrange("p (j h l) -> p h j l", j=4, l=GD),
                                             ACT.Copy, scale=scale, **extra)
                        last = nc.scalar.activation(to[:, :, o + 4 * GD:o + 5 * GD],
                                                    acc[0:rows, 3 * up + 2, bank * KW:(bank + 1) * KW].rearrange("p (h l) -> p h l", l=GD),
                                                    ACT.Copy, scale=scale, **extra)
                    last.then_inc(unit_out, 1)
            fast0 = takes(act, FAST0)
            with act.If(fast0 > 0):
                block_pairs(act, body)
                for k in range(NQ):
                    turn_out(k, 0, H - 1)

            roots(1)
            relus("lin1", yT, BS[:])
            roots(2)
            for k in range(HALVES):
                relus(f"l2h{k}", hidden[:, k], BL[:, k:k + 1])
            for k in range(HALVES):
                relus(f"l2m{k}", hid2[k], BM1[:, k:k + 1])
            roots(3)
            for q, (c0, cw) in enumerate(GROUPS):
                act.wait_ge(mm_done, filled("arow", q))
                nc.scalar.copy(arow[:, c0:c0 + cw], acc[0:P, q, 0:cw]).then_inc(ev_act, 1)
            fast = takes(act, FAST)
            act.wait_ge(l3_ready, 1)
            with act.If(fast > 0):
                for w, (groups, nacc, nct) in enumerate(SWEEPS):
                    g0 = H * sum(len(g) for g, _, _ in SWEEPS[:w])
                    ng = len(groups)
                    nblk = sum(map(len, groups))

                    def body(b, par, more, w=w, g0=g0, ng=ng, groups=groups, nacc=nacc, nct=nct, nblk=nblk):
                        B = b + H * w
                        wide_ = slice(groups[0][0] * P, (groups[0][0] + nblk) * P)
                        if isinstance(b, int) and b == 0 and w == 0:
                            pass
                        else:
                            act.wait_ge(t3_ready, B)
                        nc.scalar.activation(relu3[:, 0:nblk * P], arow[:, wide_], ACT.Relu,
                                             bias=sd[:, bass.ds(b, 1)]).then_inc(relu_ready, 1)
                        act.wait_ge(relu_ready, B + 1)
                        if not (isinstance(b, int) and b == 0 and w == 0):
                            wait(act, e3_ready, g0 + ng * (b - 1) if not isinstance(b, int) or b > 1 else g0)
                        nc.scalar.activation(t3[par][:, 0:nblk * P], relu3[:, 0:nblk * P], ACT.Exp,
                                             bias=bj[:, bass.ds(b, 1)], scale=1.0 - ALPHA).then_inc(t3_ready, 1)
                        for k in range(ng):
                            n = b * ng + (g0 + k)
                            cw = len(groups[k]) * P
                            act.wait_ge(c3_mm, n + 1)
                            wait(act, mask_used, n - ng + 1 if not isinstance(n, int) or b else g0)
                            nc.scalar.activation(mask3[k][:, 0:cw], acc[0:P, nacc + k % nct, 0:cw], ACT.Sign).then_inc(mask_ready, 1)
                    block_pairs(act, body)
                act.wait_ge(eps_in, 1)
                nc.scalar.activation(rstd[:], s_node[:, :, 0], ACT.Exp, scale=-ALPHA, bias=small[0:P, 20:21]).then_inc(eps_out, 1)
            with act.If(fast < 1):
                act.wait_ge(logits_in, 1)
                nc.scalar.activation(e_e, z_e, ACT.Exp).then_inc(logits_out, 1)
            roots(4)
            for q, (c0, cw) in enumerate(GROUPS):
                act.wait_ge(elu_in, q + 1)
                nc.scalar.activation(tmp2[:, 0:cw], tmp[:, 0:cw], ACT.Exp).then_inc(elu_exp, 1)
            roots(5)


        @block.vector
        def _(dve):
            at_chain = [dve_chain, 0]

            def link(ins):
                at_chain[1] += 1
                ins.then_inc(at_chain[0], 1)
                dve.wait_ge(*at_chain)

            branch_links = {key: 0 for key in branch_chain}

            @contextmanager
            def branch(flag, which, yes):
                outer = at_chain[:]
                at_chain[:] = [branch_chain[which, yes], branch_links[which, yes]]
                with dve.If(flag > 0 if yes else flag < 1):
                    yield
                branch_links[which, yes] = at_chain[1]
                at_chain[:] = outer

            def norm_stats(n, of):
                link(of())
                for b in range(H):
                    last = nc.vector.bn_aggr(mv[:, b, :], stats[:, b, :])
                last.then_inc(var_ready, 1)
                dve.wait_ge(std_ready, n)
                link(nc.vector.reciprocal(rstd[:], rstd[:]))

            def layer_norm(name, n, to):
                def of():
                    for q in range(NQ):
                        dve.wait_ge(mm_done, filled(name, q))
                        for j, b in enumerate(BLOCKS[q]):
                            last = nc.vector.bn_stats(stats[:, b, :], acc[0:P, q, j * D:(j + 1) * D])
                    return last
                norm_stats(n, of)
                for q in range(NQ):
                    for j, b in enumerate(BLOCKS[q]):
                        last = nc.vector.tensor_scalar(to[:, b, :], acc[0:P, q, j * D:(j + 1) * D], mv[:, b, 0:1],
                                                       rstd[:, b:b + 1], ALU.subtract, ALU.mult)
                    last.then_inc(ev_dve, 1)
                dve.wait_ge(*emptied(name, NQ - 1))

            def copies(name, to):
                for q, (c0, cw) in enumerate(GROUPS):
                    dve.wait_ge(mm_done, filled(name, q))
                    nc.vector.tensor_copy(to[:, c0:c0 + cw], acc[:, q, 0:cw]).then_inc(ev_dve, 1)
                dve.wait_ge(*emptied(name, NQ - 1))

            def add_x(name, bias):
                for q, (c0, cw) in enumerate(GROUPS):
                    dve.wait_ge(mm_done, filled(name, q))
                    nc.vector.scalar_tensor_tensor(out=yT[:, c0:c0 + cw], in0=acc[:, q, 0:cw], scalar=bias,
                                                   in1=xT[:, c0:c0 + cw], op0=ALU.add, op1=ALU.add).then_inc(ev_dve, 1)

            nc.vector.memset(ones[:], 1.0)
            nc.vector.memset(ones16[:], 1.0)
            nc.vector.memset(eps[:], LN_EPS)
            nc.vector.memset(tmp2[:, 0:1], 0.0).then_inc(prod_done, 1)
            nc.vector.memset(aggT[:], 0.0).then_inc(prod_added, NQ)
            dve.wait_ge(edges_loaded, 48)
            dve.wait_ge(consts_ready, 2)
            nc.vector.tensor_copy(ident16[:], ident[:])
            firsts = tmp[0:P, 0:EC // ROWE]
            link(nc.vector.tensor_copy(firsts, dst_i[:].rearrange("p (k r) -> p k r", r=ROWE)[:, :, 0]))
            for k in range(EC // ROWE):
                last = nc.vector.tensor_scalar(diag[:, k * P:(k + 1) * P], ident[0:P, 0:P], firsts[:, k:k + 1], None, ALU.mult)
            last.then_inc(first_ready, 1)
            dve.wait_ge(first_out, NQ)
            for t in range(GT):
                link(nc.vector.tensor_scalar(diag[:, :], frow[:, :], thr[:, t:t + 1], None, ALU.is_lt, ALU.add,
                                        accum_out=small[0:P, t:t + 1]))
            link(nc.vector.tensor_scalar(small[0:P, 8:8 + GT], small[0:P, 0:GT], -1.0, 0.0, ALU.add, ALU.max))
            nc.vector.tensor_scalar(start_i, small[0:P, 8:8 + GT], float(NROW - 1), None, ALU.min).then_inc(starts_ready, 1)
            dve.wait_ge(windows_in, 16 * 3 * GT)
            c_lo, c_key, c_wh, c_wl, c_a, c_b = cut
            link(nc.vector.tensor_copy(c_a, win_i[0]))
            link(nc.vector.tensor_scalar(c_b, c_a, 1.0 / P, -0.5 + 0.5 / P, ALU.mult, ALU.add))
            link(nc.vector.tensor_scalar(c_lo, c_b, ROUND, None, ALU.add))
            link(nc.vector.tensor_scalar(c_b, c_lo, -ROUND, None, ALU.add))
            link(nc.vector.scalar_tensor_tensor(out=c_lo, in0=c_b, scalar=-float(P), in1=c_a, op0=ALU.mult, op1=ALU.add))
            link(nc.vector.tensor_copy(c_a, win_i[1]))
            for t in range(GT):
                last = nc.vector.tensor_scalar(c_wl[:, t, :], c_a[:, t, :], thr[:, t:t + 1], None, ALU.subtract)
            link(last)
            link(nc.vector.tensor_scalar(c_wh, c_wl, float(GD - 1), None, ALU.is_le))
            link(nc.vector.scalar_tensor_tensor(out=c_a, in0=c_wl, scalar=0.0, in1=c_wh, op0=ALU.is_ge, op1=ALU.mult))
            link(nc.vector.scalar_tensor_tensor(out=c_wh, in0=c_b, scalar=float(GD), in1=c_wl, op0=ALU.mult, op1=ALU.add))
            link(nc.vector.scalar_tensor_tensor(out=c_key, in0=c_wh, scalar=KEY0, in1=c_a, op0=ALU.add, op1=ALU.mult))
            link(nc.vector.tensor_reduce(small[0:P, 16:17], c_a.rearrange("p a b -> p (a b)"), AX_X, ALU.add))
            w16 = win_i[0].rearrange("p a b -> p (a b)").bitcast(F16)[:, 0:GT * WIN].rearrange("p (a b) -> p a b", a=GT)
            link(nc.vector.tensor_scalar(w16, win_w, WS_, None, ALU.mult))
            link(nc.vector.tensor_copy(c_wh, w16))
            link(nc.vector.scalar_tensor_tensor(out=c_wl, in0=win_w, scalar=WS_, in1=c_wh, op0=ALU.mult, op1=ALU.subtract))
            nc.vector.tensor_copy(tmp2[:, 0:1], ones[:, 0:1]).then_inc(cut_ready, 1)
            w16l = win_i[1].rearrange("p a b -> p (a b)").bitcast(F16)[:, 0:GT * WIN].rearrange("p (a b) -> p a b", a=GT)
            link(nc.vector.tensor_copy(w16l, c_wl))
            link(nc.vector.tensor_tensor(c_a, c_wl, w16l, ALU.is_equal))
            link(nc.vector.scalar_tensor_tensor(out=c_b, in0=c_wh, scalar=F16_MAX, in1=c_a, op0=ALU.is_le, op1=ALU.mult))
            link(nc.vector.scalar_tensor_tensor(out=c_a, in0=c_wh, scalar=-F16_MAX, in1=c_b, op0=ALU.is_ge, op1=ALU.mult))
            nc.vector.tensor_reduce(small[0:P, 17:18], c_a.rearrange("p a b -> p (a b)"), AX_X, ALU.add).then_inc(flag_sums, 1)
            dve.wait_ge(turned_out, 4 * GT)
            dve.wait_ge(consts_ready, 3)
            dve.wait_ge(flag_mm, 1)
            link(nc.vector.tensor_scalar(small[:, 18:19], acc[:, 0, 0:1], float(E), None, ALU.is_equal))
            link(nc.vector.tensor_scalar(small[:, 19:20], acc[:, 0, 1:2], float(P * GT * WIN), None, ALU.is_equal))
            nc.vector.tensor_tensor(flag_i[:, FAST0:FAST0 + 1], small[:, 18:19], small[:, 19:20], ALU.mult).then_inc(fast0_ready, 1)
            fast0 = takes(dve, FAST0)
            fast0_f = sb_fast0
            link(nc.vector.tensor_tensor(fast0_f[:], small[:, 18:19], small[:, 19:20], ALU.mult))

            def prepare(stage):
                nc.vector.memset(zeros, 0.0)
                nc.vector.memset(ones_e, 1.0)
                nc.vector.tensor_copy(src_f, src_i[:])
                link(nc.vector.tensor_copy(dst_f, dst_i[:]))
                nc.vector.tensor_copy(tmp2[:, 0:1], ones[:, 0:1]).then_inc(prepared[stage], 1)

            def scatter(name, values, key):
                with dve.Fori(0, EC // 2) as i:
                    for k in range(2):
                        dve.wait_ge(chunk_done[name], i * 2 + (k + 1))
                        nc.vector.tensor_scalar(onehot[k], node_iota, key[:, bass.ds(i * 2 + k, 1)], None, ALU.is_equal)
                        if name in gathered:
                            dve.wait_ge(gathered[name][k], i * 16 + 16)
                        nc.vector.tensor_scalar(msg[k], rows_g[k] if name in gathered else ones[0:P, :],
                                                values[:, bass.ds(i * 2 + k, 1)], None, ALU.mult
                                                ).then_inc(msg_ready[name], 1)

            def scattered(name, to):
                for q, (c0, cw) in enumerate(GROUPS):
                    dve.wait_ge(scatter_done[name], q + 1)
                    to(slice(c0, c0 + cw), acc[:, q, 0:cw]).then_inc(scatter_out[name], 1)
                dve.wait_ge(scatter_out[name], NQ)

            def mean(c, bank):
                return nc.vector.tensor_tensor(aggT[:, c], bank, normT[:, c], ALU.mult)

            def marked(s_):
                nc.vector.tensor_copy(tmp2[:, 0:1], ones[:, 0:1]).then_inc(s_, 1)

            def hots(U, up):
                wait(dve, unit_mm, U - 1)
                lo, key, loh, lol = hot[up]
                o = bass.ds(U * UC, UC)

                def wide_(k, n):
                    return keys[k][:, o].unsqueeze(1).broadcast_to([128, n, UC])
                nc.vector.tensor_tensor(lo, iota_lo, wide_(0, 128), ALU.is_equal).then_inc(lo_ready, 1)
                nc.vector.tensor_tensor(key, iota_key, wide_(1, KW), ALU.is_equal)
                dve.wait_ge(lo_ready, U + 1)
                nc.vector.tensor_tensor(loh, lo, wide_(2, 128), ALU.mult)
                nc.vector.tensor_tensor(lol, lo, wide_(3, 128), ALU.mult).then_inc(hot_ready, 1)

            def add_product(k, bb):
                m = NQ * bb + k
                c0, cw = GROUPS[k]
                dve.wait_ge(prod_done, m + 2)
                dve.wait_ge(prod_added, m + 1)
                nc.vector.tensor_tensor(aggT[:, c0:c0 + cw], aggT[:, c0:c0 + cw], acc[:, 7, 0:cw], ALU.add).then_inc(prod_added, 1)

            with branch(fast0, FAST0, True):
                hots(0, 0)

                def body(b, par, more):
                    for u in range(UNITS):
                        if more or u < UNITS - 1:
                            hots(b * UNITS + u + 1, (par + u + 1) % 2)
                        if not (isinstance(b, int) and b == 0):
                            for k in range(NQ):
                                if P_UNIT[k] == u:
                                    add_product(k, b - 1)
                block_pairs(dve, body)
                for k in range(NQ):
                    add_product(k, H - 1)
                dve.wait_ge(prod_added, NQ + NQ * H)
                marked(sums_ready)
            with branch(fast0, FAST0, False):
                dve.wait_ge(node_iota_ready["layer0"], 1)
                prepare("layer0")
                scatter("agg0", w_e, src_f)
                scattered("agg0", lambda c, bank: nc.vector.tensor_copy(aggT[:, c], bank))
                marked(sums_ready)

            dve.wait_ge(loaded, 16 * len(loads))
            nc.vector.tensor_tensor(BS[:], BS[:], BN_[:], ALU.add)
            nc.vector.tensor_copy(A3S[:], A3[:, 0:1].broadcast_to([D, 128]))
            copies("fwd0", xT)
            add_x("lin0", B0[:])
            layer_norm("back0", 1, x)

            def parts(n):
                link(nc.vector.tensor_scalar(x16[0], x[:], XS, None, ALU.mult))
                nc.vector.scalar_tensor_tensor(out=x16[1].rearrange("p a b -> p (a b)"), in0=x[:].rearrange("p a b -> p (a b)"), scalar=XS,
                                               in1=x16[0].rearrange("p a b -> p (a b)"), op0=ALU.mult, op1=ALU.subtract).then_inc(x16_ready, 1)

            def means(layer):
                for q, (c0, cw) in enumerate(GROUPS):
                    n = NQ * layer + q
                    c = slice(c0, c0 + cw)
                    dve.wait_ge(dense_mm, n + 1)
                    if layer == 0:
                        link(nc.vector.tensor_scalar(yT[:, c], acc[:, 2 + n % 2, 0:cw], 1.0 / CS, None, ALU.mult))
                        link(nc.vector.tensor_scalar(normT[:, c], yT[:, c], 1.0, None, ALU.max))
                        link(nc.vector.reciprocal(normT[:, c], normT[:, c]))
                    nc.vector.scalar_tensor_tensor(out=aggT[:, c], in0=acc[:, n % 2, 0:cw], scalar=1.0 / (CS * XS), in1=normT[:, c],
                                                   op0=ALU.mult, op1=ALU.mult).then_inc(dense_out, 1)
            marked(x_new)
            with branch(fast0, FAST0, True):
                dve.wait_ge(c_stored[0], 16 * (H // 2 + 1))
                dve.wait_ge(c_stored[1], 16 * (H // 2))
                parts(0)
            copies("fwd1", xT)
            nc.vector.memset(small[:, 21:22], 0.0)
            with branch(fast0, FAST0, True):
                means(0)
                dve.wait_ge(dense_out, NQ)
                link(nc.vector.tensor_reduce(small[:, 20:21], yT[:], AX_X, ALU.add))
                link(nc.vector.tensor_scalar(small[:, 21:22], small[:, 20:21], float(E), None, ALU.is_equal))
            link(nc.vector.tensor_copy(tmp2[:, 1:2], ones[:, 0:1]))
            nc.vector.tensor_copy(flag_i[:, FAST:FAST + 1], small[:, 21:22]).then_inc(fast_ready, 1)
            fast = takes(dve, FAST)
            with branch(fast, FAST, True):
                marked(sums_ready)
            with branch(fast, FAST, False):
                dve.wait_ge(node_iota_ready["layers12"], 1)
                prepare("layers12")
                scatter("deg", ones_e, dst_f)
                scattered("deg", lambda c, bank: nc.vector.tensor_scalar(normT[:, c], bank, 1.0, None, ALU.max))
                link(nc.vector.reciprocal(normT[:], normT[:]))
                scatter("agg1", ones_e, dst_f)
                scattered("agg1", mean)
                marked(sums_ready)
            for q, (c0, cw) in enumerate(GROUPS):
                dve.wait_ge(*emptied("lin1", q))
                nc.vector.tensor_tensor(yT[:, c0:c0 + cw], yT[:, c0:c0 + cw], xT[:, c0:c0 + cw], ALU.add).then_inc(y1_ready, 1)
            layer_norm("back1", 2, x)
            marked(x_new)
            with branch(fast, FAST, True):
                parts(1)
            copies("fwd2", xT)
            with branch(fast, FAST, True):
                means(1)
                dve.wait_ge(dense_out, 2 * NQ)
                marked(sums_ready)
            with branch(fast, FAST, False):
                scatter("agg2", ones_e, dst_f)
                scattered("agg2", mean)
                marked(sums_ready)
            add_x("l2o", BM2[:])
            layer_norm("back2", 3, x)
            marked(x_new)
            copies("fwd3", xT)
            for q, (c0, cw) in enumerate(GROUPS):
                dve.wait_ge(mm_done, filled("h3", q))
                nc.vector.tensor_scalar(hidden[:, 0, c0:c0 + cw], acc[:, q, 0:cw], B3[:], None, ALU.add).then_inc(ev_dve, 1)
            for q in range(NQ):
                dve.wait_ge(mm_done, filled("s3", q))
                nb = len(BLOCKS[q])
                nc.vector.tensor_copy(s_node[:, q * QB:q * QB + nb, :].rearrange("p h k -> p (h k)"),
                                      acc[0:P, q, 0:2 * nb]).then_inc(ev_dve, 1)
            nc.vector.memset(hN[:, :, D:D + 1], 1.0)
            for q in range(NQ):
                dve.wait_ge(mm_done, filled("hnode", q))
                for j, b in enumerate(BLOCKS[q]):
                    last = nc.vector.tensor_copy(hN[:, b, 0:D], acc[0:P, q, j * D:(j + 1) * D])
                last.then_inc(ev_dve, 1)
            s = lambda k: small[0:P, k:k + 1]
            link(nc.vector.memset(zero3, 0.0))
            link(nc.vector.tensor_copy(sd, s_node[:, :, 1]))
            nc.vector.tensor_reduce(s(0), sd, AX_X, ALU.max).then_inc(max_in, 1)
            dve.wait_ge(*emptied("arow", NQ - 1))
            nc.vector.tensor_reduce(s(10), arow, AX_X, ALU.max)
            link(nc.vector.tensor_reduce(s(11), arow, AX_X, ALU.min))
            dve.wait_ge(max_out, 1)
            MAXS, MAXA, MINA = s(1), s(10), s(11)
            link(nc.vector.tensor_tensor(s(12), MAXS, MAXA, ALU.add))
            link(nc.vector.tensor_scalar(s(13), s(12), 0.0, 1.0 - ALPHA, ALU.max, ALU.mult))
            link(nc.vector.scalar_tensor_tensor(out=s(14), in0=MAXS, scalar=ALPHA, in1=s(13), op0=ALU.mult, op1=ALU.add))
            link(nc.vector.tensor_scalar(bj, sd, ALPHA, s(14), ALU.mult, ALU.subtract))
            link(nc.vector.tensor_scalar(s(15), MINA, -1.0, 1.0, ALU.mult, ALU.add))
            nc.vector.tensor_scalar(apos, arow, s(15), None, ALU.add).then_inc(l3_ready, 1)
            dve.wait_ge(l3_ready, 1)
            with branch(fast, FAST, True):
                for w, (groups, nacc, nct) in enumerate(SWEEPS):
                    g0 = H * sum(len(g) for g, _, _ in SWEEPS[:w])
                    ng = len(groups)
                    nblk = sum(map(len, groups))

                    def body(b, par, more, w=w, g0=g0, ng=ng, groups=groups, nacc=nacc, nct=nct, nblk=nblk):
                        B = b + H * w
                        dve.wait_ge(t3_ready, B + 1)
                        for k in range(ng):
                            n = b * ng + (g0 + k)
                            cw = len(groups[k]) * P
                            o = (groups[k][0] - groups[0][0]) * P
                            dve.wait_ge(c3_mm, n + 1)
                            wait(dve, e3_used, n - ng + 1 if not isinstance(n, int) or b else g0)
                            dve.wait_ge(mask_ready, n + 1)
                            wait(dve, mask_used, n)
                            nc.vector.tensor_tensor(e3[k][:, 0:cw], t3[par][:, o:o + cw], acc[0:P, nacc + k % nct, 0:cw],
                                                    ALU.mult).then_inc(e3_ready, 1)
                            c0 = groups[k][0] * P
                            nc.vector.tensor_tensor_reduce(junk[:, 0:cw], mask3[k][:, 0:cw], apos[:, c0:c0 + cw], 1.0, 0.0,
                                                           ALU.mult, ALU.max, rmax[par][:, k:k + 1]).then_inc(mask_used, 1)
                        dve.wait_ge(mask_used, b * ng + (g0 + ng))
                        nc.vector.tensor_copy(mx[:, bass.ds(b, 1), 4 * w:4 * w + ng], rmax[par][:, 0:ng].unsqueeze(1)).then_inc(row_done, 1)
                        dve.wait_ge(row_done, B + 1)
                    block_pairs(dve, body)
                    dve.wait_ge(sweep_done, w + 1)
                    for a in range(nacc):
                        m = min(3, nblk - 3 * a)
                        f = groups[0][0] + 3 * a
                        last = nc.vector.tensor_copy(raw3[:, f:f + m, :].rearrange("p a b -> p (a b)"), acc[0:P, a, 0:m * (D + 1)])
                    last.then_inc(sweep_out, 1)
                dve.wait_ge(sweep_out, 2)
                rows = tmp[0:P, 0:H]
                rows2 = tmp2[0:P, 0:H]
                has = tmp[0:P, H:2 * H]
                link(nc.vector.tensor_reduce(rows, mx[:, :, 0:7], AX_X, ALU.max))
                link(nc.vector.tensor_scalar(has, rows, 0.5, None, ALU.is_ge))
                link(nc.vector.tensor_tensor(rows2, rows, sd, ALU.add))
                link(nc.vector.tensor_tensor(rows, rows2, has, ALU.mult))
                link(nc.vector.tensor_scalar(rows2, has, -1.0, BIG, ALU.add, ALU.mult))
                link(nc.vector.tensor_tensor(rows, rows2, rows, ALU.add))
                nc.vector.tensor_reduce(s(2), rows, AX_X, ALU.max).then_inc(max_in, 1)
                dve.wait_ge(max_out, 2)
                link(nc.vector.tensor_tensor(s(16), s(3), s(15), ALU.subtract))
                link(nc.vector.scalar_tensor_tensor(out=s(17), in0=s(16), scalar=ALPHA, in1=s(16), op0=ALU.mult, op1=ALU.max))
                link(nc.vector.scalar_tensor_tensor(out=s(18), in0=MAXA, scalar=ALPHA, in1=s(17), op0=ALU.mult, op1=ALU.add))
                link(nc.vector.scalar_tensor_tensor(out=s(19), in0=s(12), scalar=ALPHA, in1=s(12), op0=ALU.mult, op1=ALU.max))
                nc.vector.tensor_tensor(s(20), s(18), s(19), ALU.subtract).then_inc(eps_in, 1)
                dve.wait_ge(eps_out, 1)
                link(nc.vector.scalar_tensor_tensor(out=rows, in0=rstd[:], scalar=SUM_EPS * CS, in1=raw3[:, :, D], op0=ALU.mult, op1=ALU.add))
                link(nc.vector.reciprocal(rows, rows))
                for b in range(H):
                    last = nc.vector.scalar_tensor_tensor(out=x3[:, b, :], in0=raw3[:, b, 0:D], scalar=rows[:, b:b + 1],
                                                          in1=x[:, b, :], op0=ALU.mult, op1=ALU.add)
                link(last)

            with branch(fast, FAST, False):
                prepare("layer3")
                link(nc.vector.tensor_copy(tmp2[:, 1:2], ones[:, 0:1]))
                nc.vector.tensor_copy(tmp2[:, 0:1], ones[:, 0:1]).then_inc(s_col_done, 2)
                for n in range(2):
                    with dve.Fori(0, EC // 2) as i:
                        for k in range(2):
                            dve.wait_ge(gathered[f"s{n}"][k], i * 16 + 16)
                            nc.vector.tensor_copy(s_of[n][:, bass.ds(i * 2 + k, 1)], srow[k][:, 1 - n:2 - n]).then_inc(s_col_done, 1)
                dve.wait_ge(s_col_done, 2 * EC + 2)
                link(nc.vector.tensor_tensor(s_of[0], s_of[0], s_of[1], ALU.add))
                link(nc.vector.scalar_tensor_tensor(out=z_e, in0=s_of[0], scalar=ALPHA, in1=s_of[0], op0=ALU.mult, op1=ALU.max))
                nc.vector.tensor_reduce(s(22), z_e, AX_X, ALU.max).then_inc(general_max, 1)
                dve.wait_ge(general_gmax, 1)
                nc.vector.tensor_scalar(z_e, z_e, s(23), None, ALU.subtract).then_inc(logits_in, 1)
                dve.wait_ge(logits_out, 1)
                dve.wait_ge(node_iota_ready["layer3"], 1)
                scatter("rowsum", e_e, src_f)
                scattered("rowsum", lambda c, bank: nc.vector.tensor_copy(normT[:, c], bank))
                scatter("agg3", e_e, src_f)
                scattered("agg3", lambda c, bank: nc.vector.tensor_copy(aggT[:, c], bank))
                for q, (c0, cw) in enumerate(GROUPS):
                    c = slice(c0, c0 + cw)
                    link(nc.vector.tensor_scalar(tmp[:, 0:cw], normT[:, c], SUM_EPS, None, ALU.add))
                    link(nc.vector.reciprocal(tmp2[:, 0:cw], tmp[:, 0:cw]))
                    dve.wait_ge(lin3_done, q + 1)
                    link(nc.vector.scalar_tensor_tensor(out=tmp[:, 0:cw], in0=normT[:, c], scalar=B3[:], in1=acc[:, q, 0:cw],
                                                        op0=ALU.mult, op1=ALU.add))
                    link(nc.vector.tensor_tensor(tmp[:, 0:cw], tmp[:, 0:cw], tmp2[:, 0:cw], ALU.mult))
                    nc.vector.tensor_tensor(yT[:, c], tmp[:, 0:cw], xT[:, c], ALU.add).then_inc(y3_ready, 1)
                    dve.wait_ge(y3_ready, q + 1)
                for q in range(NQ):
                    dve.wait_ge(back3_done, q + 1)
                    for j, b in enumerate(BLOCKS[q]):
                        last = nc.vector.tensor_copy(x3[:, b, :], acc[0:P, q, j * D:(j + 1) * D])
                link(last)

            def of():
                for b in range(H):
                    last = nc.vector.bn_stats(stats[:, b, :], x3[:, b, :])
                return last
            norm_stats(4, of)
            for b in range(H):
                last = nc.vector.tensor_scalar(x3[:, b, :], x3[:, b, :], mv[:, b, 0:1], rstd[:, b:b + 1], ALU.subtract, ALU.mult)
            last.then_inc(x3_ready, 1)
            for q, (c0, cw) in enumerate(GROUPS):
                c = slice(c0, c0 + cw)
                dve.wait_ge(mm_done, filled("fwd3n", q))
                link(nc.vector.tensor_scalar(yT[:, c], acc[:, q, 0:cw], G3[:], BE3[:], ALU.mult, ALU.add))
                nc.vector.tensor_scalar(tmp[:, 0:cw], yT[:, c], 0.0, None, ALU.min).then_inc(elu_in, 1)
                dve.wait_ge(elu_exp, q + 1)
                link(nc.vector.scalar_tensor_tensor(out=tmp[:, 0:cw], in0=yT[:, c], scalar=0.0, in1=tmp2[:, 0:cw],
                                                    op0=ALU.max, op1=ALU.add))
                nc.vector.scalar_tensor_tensor(out=yT[:, c], in0=tmp[:, 0:cw], scalar=-1.0, in1=xT[:, c],
                                               op0=ALU.add, op1=ALU.add).then_inc(ev_dve, 1)
                dve.wait_ge(*emptied("fwd3n", q))
            layer_norm("back4", 5, x)
            marked(x_new)
_INS = ["x", "src", "dst", "edge_weight", "L0_gnn_weight", "L0_gnn_bias", "L1_gnn_W_self", "L1_gnn_b_self",
        "L1_gnn_W_nei", "L1_gnn_b_nei", "L2_gnn_W_l", "L2_gnn_b_l", "L2_gnn_W_r", "L2_gnn_Wm1", "L2_gnn_bm1",
        "L2_gnn_Wm2", "L2_gnn_bm2", "L3_gnn_W", "L3_gnn_a", "L3_gnn_bias", "L3_gnn_gamma", "L3_gnn_beta"]
_TRANSPOSED = ("L1_gnn_W_self", "L1_gnn_W_nei")


def kernel(**inputs):
    import numpy as np
    import concourse.bacc as bacc
    from concourse.bass_utils import run_bass_kernel_spmd

    nc = bacc.Bacc("TRN2", target_bir_lowering=False, num_devices=1)
    arrays, args = {}, []
    for name in _INS:
        a = np.asarray(inputs[name])
        a = np.ascontiguousarray(a.T if name in _TRANSPOSED else a)
        arrays[f"in_{name}"] = a
        args.append(nc.dram_tensor(f"in_{name}", a.shape, mybir.dt.from_np(a.dtype), kind="ExternalInput").ap())
    out = nc.dram_tensor("out_x", inputs["x"].shape, F32, kind="ExternalOutput").ap()
    gnn_stack(nc, *args, out)
    r = run_bass_kernel_spmd(nc, [arrays], core_ids=[0])
    return r.results[0]["out_x"]
```

```python
from contextlib import ExitStack, contextmanager

import concourse.bass as bass
from concourse import mybir

ALU = mybir.AluOpType
ACT = mybir.ActivationFunctionType
AX_X = mybir.AxisListType.X
F32 = mybir.dt.float32
F16 = mybir.dt.float16
F8 = mybir.dt.float8e4
U8 = mybir.dt.uint8
I32 = mybir.dt.int32
RMAX = bass.bass_isa.ReduceOp.max

LN_EPS = 1e-5
ALPHA = 0.2
SUM_EPS = 1e-8
BIG = 1e30
ROUND = 1.5 * 2.0 ** 23


def gnn_stack(nc, x_in, src, dst, edge_weight, w0, b0, w_selfT, b_self, w_neiT, b_nei,
              w_l, b_l, w_r, wm1, bm1, wm2, bm2, w3, a3, b3, gamma, beta, out):
    N, D = x_in.shape
    E = src.shape[0]
    P = 125
    H = N // P
    EC = E // P
    QB = 4
    QW = QB * P
    GROUPS = [(q * QW, min(QW, N - q * QW)) for q in range(-(-N // QW))]
    NQ = len(GROUPS)
    BLOCKS = [list(range(q * QB, min(H, (q + 1) * QB))) for q in range(NQ)]
    HALVES = w_l.shape[1] // D
    GD = 5
    NG = N // GD
    GT = NG // P
    ROWE = 32
    WIN = 256
    WC = WIN // 128
    NROW = (E - WIN) // ROWE + 1
    UG = 5
    UC = UG * WC
    KW = H * GD
    UNITS = P // (UG * GD)
    KEY0 = 1000.0
    CS = 16.0
    WS_ = 8192.0
    XS = 1024.0
    assert H * P == N and EC * P == E and EC % 2 == 0 and D == 128 and E % ROWE == 0
    assert GT * P == NG and UNITS * UG * GD == P and H % 2 == 1

    with ExitStack() as ctx:
        def sb(name, shape, dt=F32):
            return ctx.enter_context(nc.sbuf_tensor(name, shape, dt))

        def sem(name):
            return ctx.enter_context(nc.semaphore(name))

        acc = ctx.enter_context(nc.psum_tensor("acc", [128, 8, 512], F32))

        x = sb("x", [P, H, D])
        xT = sb("xT", [128, N])
        aggT = sb("aggT", [128, N])
        normT = sb("normT", [128, N])
        yT = sb("yT", [128, N])
        hidden = sb("hidden", [128, HALVES, N])
        x3 = sb("x3", [P, H, D])
        hid2 = [aggT, yT]
        src_i = sb("src_i", [P, EC], I32)
        dst_i = sb("dst_i", [P, EC], I32)
        w_e = sb("w_e", [P, EC])
        ident = sb("ident", [128, 128])
        ident16 = sb("ident16", [128, 128], F16)
        ones = sb("ones", [128, 128])
        ones16 = sb("ones16", [128, 128], F16)
        eps = sb("eps", [128, 1])
        W0, WS, WN, W3 = sb("W0", [D, D]), sb("WS", [D, D]), sb("WN", [D, D]), sb("W3", [D, D])
        WL, WR = sb("WL", [D, HALVES * D]), sb("WR", [D, HALVES * D])
        WM1 = sb("WM1", [D, HALVES, HALVES * D])
        WM2 = sb("WM2", [D, HALVES, D])
        A3 = sb("A3", [D, 2])
        A3S = sb("A3S", [D, 128])
        B0, BS, BN_, B3, G3, BE3, BM2 = (sb(n, [D, 1]) for n in ("B0", "BS", "BN", "B3", "G3", "BE3", "BM2"))
        BL, BM1 = sb("BL", [D, HALVES]), sb("BM1", [D, HALVES])
        stats = sb("stats", [P, H, 6])
        mv = sb("mv", [P, H, 2])
        rstd = sb("rstd", [P, H])
        shift = sb("shift", [P, H])
        ideg = sb("ideg", [P, GT * GD])
        s_node = sb("s_node", [P, H, 2])
        small = sb("small", [128, 64])
        tmp = sb("tmp", [128, QW])
        tmp2 = sb("tmp2", [128, QW])
        flag_i = sb("flag_i", [128, 2], I32)
        FAST0, FAST = 0, 1

        ARENA = 85 * 1024
        arena = sb("arena", [128, ARENA], U8)
        at = [0]

        def tile(shape, dt=F32):
            size = {F32: 4, I32: 4, F16: 2, U8: 1}[dt]
            n = 1
            for d in shape[1:]:
                n *= d
            flat = arena[0:shape[0], at[0]:at[0] + n * size].bitcast(dt)
            at[0] += -(-n * size // 32) * 32
            assert at[0] <= ARENA, at[0]
            if len(shape) == 2:
                return flat
            names = "abc"[:len(shape) - 1]
            return flat.rearrange(f"p ({' '.join(names)}) -> p {' '.join(names)}",
                                  **{k: v for k, v in zip(names[1:], shape[2:])})

        keys = [tile([128, NG * WC], F16) for _ in range(4)]
        iota_lo = tile([128, P, UC], F16)
        iota_key = tile([128, KW, UC], F16)
        build_at = at[0]
        win_i = [tile([P, GT, WIN], I32) for _ in range(2)]
        win_w = tile([P, GT, WIN])
        cut = [tile([P, GT, WIN]) for _ in range(6)]
        within = yT[0:P, 0:GT * WIN].rearrange("p (t w) -> p t w", w=WIN)
        diag = hidden[0:P, 0, :]
        frow = hidden[0:P, 1, :]
        thr = tile([P, GT])
        thr_bias = tile([P, GT])
        start_i = tile([P, GT], I32)
        at[0] = build_at
        hot = [[tile([128, P, UC], F16), tile([128, KW, UC], F16), tile([128, P, UC], F16), tile([128, P, UC], F16)]
               for _ in range(2)]
        c_stage = [tile([128, H, P], U8) for _ in range(2)]
        strip = [[tile([P, H, P]), x3[:, :, 0:P]],
                 [hidden[0:P, k, :].rearrange("p (h l) -> p h l", l=P) for k in range(2)]]
        wblk = [[tile([P, QW]) for _ in range(2)] for _ in range(2)]
        xb = [[tile([P, D]) for _ in range(2)] for _ in range(2)]
        at[0] = 0
        cb = [tile([128, QB, N], U8) for _ in range(2)]
        x16 = [tile([P, H, D], F16) for _ in range(2)]
        at[0] = 0
        SWEEPS = [(0, [(6, 3, (3, 5)), (3, 3, (7, 7))]),
                  (9, [(8, 4, (3, 5))]),
                  (17, [(8, 4, (3, 5))])]
        NS = len(SWEEPS)
        SUM_BANKS = 3
        SWW = max(sum(n for n, _, _ in pieces) for _, pieces in SWEEPS) * P
        assert sum(n for _, pieces in SWEEPS for n, _, _ in pieces) == H
        c3 = [tile([128, SWW], U8) for _ in range(4)]
        relu3 = [tile([P, SWW]) for _ in range(2)]
        hN = tile([P, H, D + 2])
        raw3 = tile([P, H, D + 1])
        e3 = [tile([P, SWW]) for _ in range(2)]
        zero3 = tile([P, 3 * (D + 1)])
        arow = hidden[0:P, 1, :]
        urow = aggT[0:P, :]
        smax = yT[0:P, :]
        sd = small[0:P, 32:32 + H]
        sp_ = x3[:, 2, 32:32 + H]
        bj = x3[:, 0, 0:H]
        vj = x3[:, 0, 32:32 + H]
        kj = x3[:, 1, 0:H]
        nkj = x3[:, 1, 32:32 + H]
        evj = x3[:, 2, 0:H]

        at[0] = 0
        node_iota = tile([P, N])
        onehot = [tile([P, N]) for _ in range(2)]
        src_f, dst_f, ones_e, z_e, e_e = (tile([P, EC]) for _ in range(5))
        s_of = [tile([P, EC]) for _ in range(2)]
        zeros = tile([P, QW])
        gidx = [tile([P, 1], I32) for _ in range(2)]
        rows_g = [tile([P, D]) for _ in range(2)]
        srow = [tile([P, 2]) for _ in range(2)]
        msg = [tile([P, D]) for _ in range(2)]
        pause = tile([P, 1])
        tables = [x_in] + [nc.dram_tensor(f"x{n}_table", [N, D], F32, kind="Internal").ap() for n in (1, 2, 3)]
        s_table = nc.dram_tensor("s_table", [N, 2], F32, kind="Internal").ap()
        PASSES = ["agg0", "deg", "agg1", "agg2", "rowsum", "agg3"]

        deg_dram = nc.dram_tensor("inverse_degrees", [N], F32, kind="Internal").ap()
        c_dram = nc.dram_tensor("counts", [H, 128, N], U8, kind="Internal").ap()

        loaded = sem("loaded")
        edges_loaded = sem("edges_loaded")
        dst_loaded = sem("dst_loaded")
        counted = sem("counted")
        count_bias = sem("count_bias")
        consts_ready = sem("consts_ready")
        dve_chain = sem("dve_chain")
        branch_chain = {(which, yes): sem(f"dve_chain_{which}_{yes}") for which in (FAST0, FAST) for yes in (True, False)}
        first_ready = sem("first_ready")
        first_mm = sem("first_mm")
        first_out = sem("first_out")
        starts_ready = sem("starts_ready")
        windows_in = sem("windows_in")
        weights_in = sem("weights_in")
        cut_ready = sem("cut_ready")
        turned = sem("turned")
        turned_out = sem("turned_out")
        hot_ready = sem("hot_ready")
        lo_ready = sem("lo_ready")
        stage_clear = sem("stage_clear")
        x3_ready = sem("x3_ready")
        x3_late = sem("x3_late")
        unit_mm = sem("unit_mm")
        unit_out = sem("unit_out")
        c_stored = [sem(f"c_stored{k}") for k in range(2)]
        xb_loaded = [sem(f"xb_loaded{k}") for k in range(2)]
        wt_done = sem("wt_done")
        wblk_ready = sem("wblk_ready")
        prod_done = sem("prod_done")
        prod_added = sem("prod_added")
        x16_ready = sem("x16_ready")
        cb_loaded = [sem(f"cb_loaded{k}") for k in range(2)]
        dense_mm = sem("dense_mm")
        dense_out = sem("dense_out")
        mm_done = sem("mm_done")
        ev_dve = sem("ev_dve")
        ev_act = sem("ev_act")
        x_loaded = sem("x_loaded")
        xt_mm = sem("xt_mm")
        xt_out = sem("xt_out")
        deg_ready = sem("deg_ready")
        deg_stored = sem("deg_stored")
        deg_loaded = sem("deg_loaded")
        bias_ready = sem("bias_ready")
        var_ready = sem("var_ready")
        std_ready = sem("std_ready")
        elu_in = sem("elu_in")
        elu_min = sem("elu_min")
        elu_exp = sem("elu_exp")
        y1_ready = sem("y1_ready")
        x_new = sem("x_new")
        max_in = sem("max_in")
        max_out = sem("max_out")
        l3_ready = sem("l3_ready")
        c3_loaded = [sem(f"c3_loaded{k}") for k in range(4)]
        c3_mm = [sem(f"c3_mm{k}") for k in range(2)]
        e3_ready = [sem(f"e3_ready{k}") for k in range(2)]
        piece_max = [sem(f"piece_max{k}") for k in range(2)]
        relu_ready = sem("relu_ready")
        scalars_ready = sem("scalars_ready")
        exps_ready = sem("exps_ready")
        e3_used = sem("e3_used")
        sweep_done = sem("sweep_done")
        sweep_out = sem("sweep_out")
        eps_in = sem("eps_in")
        eps_out = sem("eps_out")
        out_stored = sem("out_stored")
        flag_sums = sem("flag_sums")
        flag_mm = sem("flag_mm")
        fast0_ready = sem("fast0_ready")
        fast_ready = sem("fast_ready")
        sums_ready = sem("sums_ready")
        STAGES = ("layer0", "layers12", "layer3")
        prepared = {p: sem(f"prepared_{p}") for p in STAGES}
        node_iota_ready = {p: sem(f"node_iota_ready_{p}") for p in STAGES}
        table_ready = [sem(f"table_ready{n}") for n in range(4)]
        s_table_ready = sem("s_table_ready")
        gidx_ready = {p: sem(f"gidx_ready_{p}") for p in ("agg0", "agg1", "agg2", "agg3", "s0", "s1")}
        gathered = {p: [sem(f"gathered_{p}_{k}") for k in range(2)] for p in gidx_ready}
        msg_ready = {p: sem(f"msg_ready_{p}") for p in PASSES}
        chunk_done = {p: sem(f"chunk_done_{p}") for p in PASSES}
        scatter_done = {p: sem(f"scatter_done_{p}") for p in PASSES}
        scatter_out = {p: sem(f"scatter_out_{p}") for p in PASSES}
        s_col_done = sem("s_col_done")
        general_max = sem("general_max")
        general_gmax = sem("general_gmax")
        logits_in = sem("logits_in")
        logits_out = sem("logits_out")
        lin3_done = sem("lin3_done")
        y3_ready = sem("y3_ready")
        back3_done = sem("back3_done")

        DQ = NQ // 2 + 1
        XC = 2 * QB
        NX = -(-H // XC)
        dve_all, act_all = [ev_dve] * NQ, [ev_act] * NQ
        both = [(ev_dve, ev_act)[q % 2] for q in range(NQ)]
        ROUNDS = [("lin0", dve_all), ("back0", both), ("fwd1", act_all),
                  ("lin1", act_all), ("back1", both), ("fwd2", act_all),
                  ("l2h0", both), ("l2h1", both), ("l2m0", both), ("l2m1", both), ("l2o", dve_all),
                  ("back2", both), ("fwd3", both),
                  ("h3", both), ("s3", dve_all), ("arow", act_all), ("hnode", dve_all),
                  ("fwd3n", dve_all), ("back4", both)]
        NUMBER = {name: n for n, (name, _) in enumerate(ROUNDS)}

        def filled(name, q):
            return NQ * NUMBER[name] + q + 1

        def emptied(name, q):
            n = NUMBER[name]
            s = ROUNDS[n][1][q]
            return s, sum(1 for _, by in ROUNDS[:n] for t in by if t is s) + sum(1 for t in ROUNDS[n][1][:q + 1] if t is s)

        def all_emptied(eng, name):
            eng.wait_ge(*emptied(name, NQ - 1))
            eng.wait_ge(*emptied(name, NQ - 2))

        def shares(name, s):
            return [(q, *GROUPS[q]) for q in range(NQ) if ROUNDS[NUMBER[name]][1][q] is s]

        def takes(eng, which):
            eng.wait_ge(fast0_ready if which == FAST0 else fast_ready, 1)
            return eng.value_load(flag_i[0:1, which:which + 1], min_val=0, max_val=1)

        def wait(eng, s, value):
            if not isinstance(value, int) or value > 0:
                eng.wait_ge(s, value)

        PAIRS = H // 2
        TURNS = 2 * NQ

        def turn_slots(units):
            return {int((units * UG - 2) * t / TURNS) + 1: t for t in range(TURNS)}

        def turns_in(units, u):
            return [t for g, t in sorted(turn_slots(units).items()) if g // UG == u]

        def product_slots(units):
            return {g: t // 2 - 1 for g, t in turn_slots(units).items() if t and t % 2 == 0}

        def adds_in(units, u):
            place = {k: g for g, k in product_slots(units).items()}
            return [k for k in range(NQ) if min(units - 1, (place[k] + 2) // UG if k in place else units - 1) == u]

        def last_block(p):
            return isinstance(p, int) and p == PAIRS

        def tail_banks(k):
            return ((6, 7), (4, 5))[k % 2]

        loads = [(W0[:], w0), (WS[:], w_selfT), (WN[:], w_neiT), (W3[:], w3), (WL[:], w_l), (WR[:], w_r),
                 (WM1[:], wm1.rearrange("(k p) n -> p k n", p=D)),
                 (WM2[:], wm2.rearrange("(k p) n -> p k n", p=D)),
                 (A3[:], a3.rearrange("(k p) -> p k", p=D)),
                 (BL[:], b_l.rearrange("(k p) -> p k", p=D)),
                 (BM1[:], bm1.rearrange("(k p) -> p k", p=D)),
                 ] + [(t[:], v.rearrange("(p k) -> p k", k=1)) for t, v in
                      ((B0, b0), (BS, b_self), (BN_, b_nei), (B3, b3), (G3, gamma), (BE3, beta), (BM2, bm2))]

        TILE_ORDER = [2, 0, 3, 1, 4]
        ACT_TILES = [2, 3, 4]
        assert sorted(TILE_ORDER) == list(range(GT)) and E // ROWE == N

        def each_pair(eng, body):
            body(0, 0, 2)
            body(1, 1, 2)
            with eng.Fori(0, PAIRS // 2 - 1) as i:
                body(i * 2 + 2, 0, 2)
                body(i * 2 + 3, 1, 2)
            body(PAIRS, 0, 1)
        assert GT == UNITS
        assert PAIRS % 2 == 0 and UNITS * 2 % 2 == 0

        def block_fours(eng, body):
            for b in range(3):
                body(b, b)
            with eng.Fori(0, (H - 5) // 4) as i:
                for u in range(4):
                    body(i * 4 + (3 + u), (3 + u) % 4)
            body(H - 2, (H - 2) % 4)
            body(H - 1, (H - 1) % 4)
        assert H % 4 == 1

        block = ctx.enter_context(nc.Block())

        @block.sync
        def _(sp):
            for to, frm, s_ in ((dst_i, dst, dst_loaded), (src_i, src, edges_loaded), (w_e, edge_weight, edges_loaded)):
                sp.dma_start(to[:], frm.rearrange("(p c) -> p c", p=P)).then_inc(s_, 16)
            sp.dma_start(x[:], x_in.rearrange("(h p) d -> p h d", p=P)).then_inc(x_loaded, 16)
            with nc.allow_non_contiguous_dma(reason="a bias per feature: 128 short runs each"):
                for to, frm in loads:
                    sp.dma_start(to, frm).then_inc(loaded, 16)

            fast0 = takes(sp, FAST0)
            with sp.If(fast0 > 0):
                sp.wait_ge(turned_out, 4 * GT)
                def body(p, qp, blocks):
                    if not isinstance(p, int) or p > 1:
                        sp.wait_ge(prod_done, NQ * (p - 1) + 1)
                    for k in range(blocks):
                        b = p * 2 + k
                        sp.wait_ge(unit_out, UNITS * (b + 1))
                        sp.dma_start(xb[qp][k][:], x_in[bass.ds(b * P, P), :]).then_inc(xb_loaded[qp], 16)
                        sp.dma_start(c_dram[bass.ds(b, 1)].rearrange("a p f -> p (a f)"),
                                     c_stage[k].rearrange("p a b -> p (a b)")).then_inc(c_stored[k], 16)
                each_pair(sp, body)
                sp.wait_ge(c_stored[0], 16 * (H // 2 + 1))
                sp.wait_ge(c_stored[1], 16 * (H // 2))
                sp.wait_ge(deg_ready, 1)
                with nc.allow_non_contiguous_dma(reason="the degrees of a group: 625 short runs"):
                    sp.dma_start(deg_dram.rearrange("(t p l) -> p t l", p=P, l=GD),
                                 ideg[:].rearrange("p (t l) -> p t l", l=GD)).then_inc(deg_stored, 16)
                sp.wait_ge(deg_stored, 16)
                sp.dma_start(normT[:], deg_dram.rearrange("(a n) -> a n", a=1).broadcast_to([128, N])).then_inc(deg_loaded, 16)
                sp.wait_ge(prod_added, NQ * (PAIRS + 2))

            def load_counts(layer):
                for q, (c0, cw) in enumerate(GROUPS):
                    n = NQ * layer + q
                    wait(sp, dense_mm, n - 1)
                    nb = len(BLOCKS[q])
                    sp.dma_start(cb[n % 2][:, 0:nb, :],
                                 c_dram[q * QB:q * QB + nb].rearrange("b p f -> p b f")).then_inc(cb_loaded[n % 2], 16)

            def store_table(layer):
                sp.wait_ge(x_new, layer)
                sp.dma_start(tables[layer].rearrange("(h p) d -> p h d", p=P), x[:]).then_inc(table_ready[layer], 16)
                sp.wait_ge(table_ready[layer], 16)

            with sp.If(fast0 > 0):
                load_counts(0)
            fast = takes(sp, FAST)
            with sp.If(fast > 0):
                load_counts(1)
                sp.wait_ge(dense_mm, 2 * NQ)
                for w, (first, pieces) in enumerate(SWEEPS):
                    width = sum(n for n, _, _ in pieces) * P

                    def body(b, ph, w=w, first=first, width=width):
                        if not isinstance(b, int) or b > 3:
                            sp.wait_ge(c3_mm[0], b + (H * w - 3))
                            if w == 0:
                                sp.wait_ge(c3_mm[1], b - 3)
                        elif w:
                            older = (H - 1) // 4 * 4 + ph - (4 if ph else 0)
                            sp.wait_ge(c3_mm[0], H * (w - 1) + older + 1)
                            if w == 1:
                                sp.wait_ge(c3_mm[1], older + 1)
                        sp.dma_start(c3[ph][:, 0:width],
                                     c_dram[bass.ds(b, 1), :, first * P:first * P + width].rearrange("a p f -> p (a f)")
                                     ).then_inc(c3_loaded[ph], 16)
                    block_fours(sp, body)
            with sp.If(fast < 1):
                for layer in (1, 2, 3):
                    store_table(layer)
                sp.wait_ge(l3_ready, 1)
                sp.dma_start(s_table.rearrange("(h p) k -> p h k", p=P), s_node[:]).then_inc(s_table_ready, 16)
                sp.wait_ge(s_table_ready, 16)
            sp.wait_ge(x_new, 4)
            sp.dma_start(out.rearrange("(h p) d -> p h d", p=P), x[:]).then_inc(out_stored, 16)
            sp.wait_ge(out_stored, 16)

        @block.gpsimd
        def _(pool):
            nc.gpsimd.memset(ident[:], 0.0).then_inc(consts_ready, 1)
            pool.wait_ge(consts_ready, 1)
            nc.gpsimd.affine_select(out=ident[:], in_=ident[:], compare_op=ALU.not_equal, fill=1.0, base=0,
                                    pattern=[[-1, 128]], channel_multiplier=1)
            nc.gpsimd.iota(thr, [[GD * P, GT]], base=0, channel_multiplier=GD,
                           allow_small_or_imprecise_dtypes=True).then_inc(consts_ready, 1)
            nc.gpsimd.iota(iota_lo, [[1, P], [0, UC]], base=0, channel_multiplier=0,
                           allow_small_or_imprecise_dtypes=True)
            nc.gpsimd.iota(iota_key, [[1, KW], [0, UC]], base=int(KEY0), channel_multiplier=0,
                           allow_small_or_imprecise_dtypes=True).then_inc(consts_ready, 1)
            def windows(t, to, frm, landed):
                nc.gpsimd.indirect_dma_start(out=to[:, t, :], out_offset=None, in_=frm.rearrange("(e k) -> e k", k=1),
                                             in_offset=bass.IndirectOffsetOnAxis(start_i[:, t:t + 1], 0)
                                             ).then_inc(landed, 16)
            for n, t in enumerate(TILE_ORDER):
                pool.wait_ge(starts_ready, n + 1)
                windows(t, win_i[0], src, windows_in)
                windows(t, win_i[1], dst, windows_in)
            for t in range(GT):
                windows(t, win_w, edge_weight, weights_in)

            def gather(name, idx, table, to, free, first):
                with pool.Fori(0, EC // 2) as i:
                    for k in range(2):
                        pool.wait_ge(free, i * 2 + (first + k + 1))
                        nc.gpsimd.tensor_copy(gidx[k], idx[:, bass.ds(i * 2 + k, 1)]).then_inc(gidx_ready[name], 1)
                        pool.wait_ge(gidx_ready[name], i * 2 + (k + 1))
                        nc.gpsimd.tensor_tensor(pause, ident[0:P, 0:1], ident[0:P, 0:1], ALU.add)
                        nc.gpsimd.indirect_dma_start(out=to[k], out_offset=None, in_=table,
                                                     in_offset=bass.IndirectOffsetOnAxis(gidx[k][:, 0:1], 0)
                                                     ).then_inc(gathered[name][k], 16)

            def node_indices(stage):
                nc.gpsimd.iota(node_iota, [[1, N]], base=0, channel_multiplier=0,
                               allow_small_or_imprecise_dtypes=True).then_inc(node_iota_ready[stage], 1)

            fast0 = takes(pool, FAST0)
            with pool.If(fast0 > 0):
                pool.wait_ge(turned_out, 4 * GT)
                for k in range(2):
                    last = nc.gpsimd.memset(c_stage[k], 0)
                last.then_inc(stage_clear, 1)
            with pool.If(fast0 < 1):
                node_indices("layer0")
                gather("agg0", dst_i, tables[0], rows_g, chunk_done["agg0"], 0)
            fast = takes(pool, FAST)
            with pool.If(fast < 1):
                node_indices("layers12")
                for layer in (1, 2):
                    pool.wait_ge(table_ready[layer], 16)
                    gather(f"agg{layer}", src_i, tables[layer], rows_g, chunk_done[f"agg{layer}"], 0)
            pool.wait_ge(max_in, 1)
            nc.gpsimd.partition_all_reduce(small[0:P, 8:11], small[0:P, 4:7], P, RMAX).then_inc(max_out, 1)
            with pool.If(fast > 0):
                pool.wait_ge(max_in, 2)
                nc.gpsimd.partition_all_reduce(small[0:P, 3:4], small[0:P, 2:3], P, RMAX).then_inc(max_out, 1)
            with pool.If(fast < 1):
                pool.wait_ge(l3_ready, 1)
                node_indices("layer3")
                pool.wait_ge(s_table_ready, 16)
                for k, idx in enumerate((dst_i, src_i)):
                    gather(f"s{k}", idx, s_table, srow, s_col_done, EC * k)
                pool.wait_ge(general_max, 1)
                nc.gpsimd.partition_all_reduce(small[0:P, 23:24], small[0:P, 22:23], P, RMAX).then_inc(general_gmax, 1)
                pool.wait_ge(table_ready[3], 16)
                gather("agg3", dst_i, tables[3], rows_g, chunk_done["agg3"], 0)

        @block.tensor
        def _(pe):
            def fill(name, steps):
                before = ROUNDS[NUMBER[name] - 1][0] if NUMBER[name] else None
                for q, (c0, cw) in enumerate(GROUPS):
                    if before:
                        pe.wait_ge(*emptied(before, q))
                    steps(q, c0, cw).then_inc(mm_done, 1)

            def x_turn(k):
                if k:
                    pe.wait_ge(xt_out, k)
                for j, h in enumerate(BLOCKS[k]):
                    last = nc.tensor.transpose(acc[:, 6, j * P:(j + 1) * P], x[:, h, :], ident[0:P, 0:P])
                last.then_inc(xt_mm, 1)

            def to_nodes(name, frm):
                def steps(q, c0, cw):
                    for j, b in enumerate(BLOCKS[q]):
                        last = nc.tensor.transpose(acc[0:P, q, j * D:(j + 1) * D], frm[:, b * P:(b + 1) * P], ident[:])
                    return last
                fill(name, steps)

            def to_features(name, frm):
                def steps(q, c0, cw):
                    for j, b in enumerate(BLOCKS[q]):
                        last = nc.tensor.transpose(acc[:, q, j * P:(j + 1) * P], frm[:, b, :], ident[0:P, 0:P])
                    return last
                fill(name, steps)

            def linear(name, terms):
                def steps(q, c0, cw):
                    for n, (w, v) in enumerate(terms):
                        last = nc.tensor.matmul(acc[:, q, 0:cw], w, v[:, c0:c0 + cw],
                                                start=(n == 0), stop=(n == len(terms) - 1))
                    return last
                fill(name, steps)

            def dense_sums(layer):
                for q, (c0, cw) in enumerate(GROUPS):
                    n = NQ * layer + q
                    nb = len(BLOCKS[q])
                    pe.wait_ge(cb_loaded[n % 2], 16 * (n // 2 + 1))
                    wait(pe, dense_out, n - 1)
                    for h in range(H):
                        if q == 0 and h % XC == 0:
                            pe.wait_ge(x16_ready, NX * layer + h // XC + 1)
                        rhs = cb[n % 2].bitcast(F8)[0:P, 0:nb, h * P:(h + 1) * P]
                        for part in range(2):
                            last = nc.tensor.matmul(acc[:, n % 2, 0:cw], x16[part][:, h, :], rhs,
                                                    start=(h == 0 and part == 0), stop=(h == H - 1 and part == 1))
                    last.then_inc(dense_mm, 1)

            def scatter(name):
                for q, (c0, cw) in enumerate(GROUPS):
                    last = nc.tensor.matmul(acc[:, q, 0:cw], zeros[:, 0:D], zeros[:, 0:cw], start=True, stop=False)
                last.then_inc(chunk_done[name], 2)
                with pe.Fori(0, EC // 2) as i:
                    for k in range(2):
                        pe.wait_ge(msg_ready[name], i * 2 + (k + 1))
                        for q, (c0, cw) in enumerate(GROUPS):
                            last = nc.tensor.matmul(acc[:, q, 0:cw], msg[k], onehot[k][:, c0:c0 + cw],
                                                    start=False, stop=False)
                        last.then_inc(chunk_done[name], 1)
                for q, (c0, cw) in enumerate(GROUPS):
                    nc.tensor.matmul(acc[:, q, 0:cw], zeros[:, 0:D], zeros[:, 0:cw],
                                     start=False, stop=True).then_inc(scatter_done[name], 1)

            pe.wait_ge(first_ready, 1)
            for q, (c0, cw) in enumerate(GROUPS):
                nc.tensor.matmul(acc[0:P, q, 0:cw], ones[0:P, 0:P], diag[:, c0:c0 + cw],
                                 start=True, stop=True).then_inc(first_mm, 1)
            pe.wait_ge(first_out, NQ)
            n = 0
            for k in range(4):
                v = cut[k]
                pe.wait_ge(cut_ready, k + 1)
                for t in range(GT):
                    wait(pe, turned_out, n - 7)
                    for h in range(WC):
                        last = nc.tensor.transpose(acc[:, n % 8, h * P:(h + 1) * P], v[:, t, h * 128:(h + 1) * 128],
                                                   ident[0:P, 0:P])
                    last.then_inc(turned, 1)
                    n += 1
            pe.wait_ge(turned_out, n)
            pe.wait_ge(x_loaded, 16)
            pe.wait_ge(flag_sums, 1)
            nc.tensor.matmul(acc[:, 0, 0:2], ones[0:P, :], small[0:P, 16:18], start=True, stop=True).then_inc(flag_mm, 1)
            fast0 = takes(pe, FAST0)

            def turn_step(p, qp, t, n, bank=6):
                pe.wait_ge(unit_out, UNITS * (p * 2 + (t % 2 + 1)))
                wait(pe, wblk_ready, n - 1 if last_block(p) and t else n)
                for j, h in enumerate(BLOCKS[t // 2]):
                    last = nc.tensor.transpose(acc[0:P, bank, j * P:(j + 1) * P], strip[qp][t % 2][:, h, :], ident[0:P, 0:P])
                last.then_inc(wt_done, 1)

            def product_step(p, qp, k, parts, n, bank=7):
                c0, cw = GROUPS[k]
                if k == 0:
                    pe.wait_ge(xb_loaded[qp], p // 2 * 32 + 16 * len(parts) if isinstance(p, int) else (p - qp) * 16 + 32)
                pe.wait_ge(wblk_ready, n)
                pe.wait_ge(prod_added, NQ * (p + 1) + k - (1 if last_block(p) and k else 0))
                for m, (xb_, w_) in enumerate(parts):
                    last = nc.tensor.matmul(acc[:, bank, 0:cw], xb_, w_[:, 0:cw], start=(m == 0), stop=(m == len(parts) - 1))
                last.then_inc(prod_done, 1)

            def pair_product(p, qp, k):
                product_step(p, qp, k, [(xb[qp][m][:], wblk[k % 2][m]) for m in range(2)], TURNS * p + 2 * k + 2)

            def body(p, qp, blocks):
                units = blocks * UNITS
                slots = turn_slots(units)
                first = isinstance(p, int) and p == 0
                for g in range(units * UG):
                    u, j = divmod(g, UG)
                    up = u % 2
                    if j == 0:
                        U = p * (2 * UNITS) + u
                        pe.wait_ge(hot_ready, U + 1)
                        wait(pe, unit_out, U - 1)
                    lo, key, loh, lol = hot[up]
                    cbank = acc[0:P, 3 * up, j * KW:(j + 1) * KW] if j < 4 else acc[0:P, 3 * up + 2, 0:KW]
                    wbank = acc[0:P, 3 * up + 1, j * KW:(j + 1) * KW] if j < 4 else acc[0:P, 3 * up + 2, KW:2 * KW]
                    for c in range(WC):
                        cc = j * WC + c
                        nc.tensor.matmul(cbank, lo[:, :, cc], key[:, :, cc], start=(c == 0), stop=(c == WC - 1))
                    for c in range(WC):
                        cc = j * WC + c
                        nc.tensor.matmul(wbank, loh[:, :, cc], key[:, :, cc], start=(c == 0), stop=False)
                        last = nc.tensor.matmul(wbank, lol[:, :, cc], key[:, :, cc], start=False, stop=(c == WC - 1))
                    if j == UG - 1:
                        last.then_inc(unit_mm, 1)
                    if g in slots and first and slots[g] % 2 == 0:
                        x_turn(slots[g] // 2)
                    if g in slots and not first:
                        t = slots[g]
                        if isinstance(p, int) and p == 1 and t == 0:
                            pe.wait_ge(xt_out, NQ)
                        turn_step(p - 1, 1 - qp, t, TURNS * (p - 1) + t)
                    if g in product_slots(units) and not first:
                        pair_product(p - 1, 1 - qp, product_slots(units)[g])
                if not first:
                    pair_product(p - 1, 1 - qp, NQ - 1)
            with pe.If(fast0 > 0):
                each_pair(pe, body)
                turn_step(PAIRS, 0, 0, TURNS * PAIRS, tail_banks(0)[0])
                for k in range(NQ):
                    n = TURNS * PAIRS + k
                    if k + 1 < NQ:
                        turn_step(PAIRS, 0, 2 * k + 2, n + 1, tail_banks(k + 1)[0])
                    product_step(PAIRS, 0, k, [(xb[0][0][:], wblk[k % 2][0])], n + 1, tail_banks(k)[1])
            with pe.If(fast0 < 1):
                for k in range(NQ):
                    x_turn(k)
                pe.wait_ge(prepared["layer0"], 1)
                pe.wait_ge(xt_out, NQ)
                scatter("agg0")

            pe.wait_ge(sums_ready, 1)
            pe.wait_ge(loaded, 16 * len(loads))
            linear("lin0", [(W0[:], aggT)])
            to_nodes("back0", yT)
            to_features("fwd1", x)
            pe.wait_ge(*emptied("fwd1", 1))
            with pe.If(fast0 > 0):
                dense_sums(0)
            fast = takes(pe, FAST)
            with pe.If(fast < 1):
                pe.wait_ge(prepared["layers12"], 1)
                all_emptied(pe, "fwd1")
                scatter("deg")
                pe.wait_ge(scatter_out["deg"], NQ)
                scatter("agg1")
            pe.wait_ge(sums_ready, 2)
            linear("lin1", [(WS[:], xT), (WN[:], aggT)])
            pe.wait_ge(y1_ready, NQ)
            to_nodes("back1", yT)
            to_features("fwd2", x)
            pe.wait_ge(*emptied("fwd2", 1))
            with pe.If(fast > 0):
                dense_sums(1)
            with pe.If(fast < 1):
                all_emptied(pe, "fwd2")
                scatter("agg2")
            pe.wait_ge(sums_ready, 3)
            for k in range(HALVES):
                c = slice(k * D, (k + 1) * D)
                linear(f"l2h{k}", [(WL[:, c], aggT), (WR[:, c], xT)])
            for k in range(HALVES):
                c = slice(k * D, (k + 1) * D)
                linear(f"l2m{k}", [(WM1[:, j, c], hidden[:, j]) for j in range(HALVES)])
            linear("l2o", [(WM2[:, j, :], hid2[j]) for j in range(HALVES)])
            to_nodes("back2", yT)
            to_features("fwd3", x)
            linear("h3", [(W3[:], xT)])

            def node_terms(q, c0, cw):
                for j, b in enumerate(BLOCKS[q]):
                    last = nc.tensor.matmul(acc[0:P, q, 2 * j:2 * j + 2], hidden[:, 0, b * P:(b + 1) * P], A3[:],
                                            start=True, stop=True)
                return last
            fill("s3", node_terms)
            linear("arow", [(A3S[:], hidden[:, 0])])
            to_nodes("hnode", hidden[:, 0])
            pe.wait_ge(l3_ready, 1)
            with pe.If(fast > 0):
                for w, (first, pieces) in enumerate(SWEEPS):
                    nblk = sum(n for n, _, _ in pieces)
                    starts = [sum(n for n, _, _ in pieces[:k]) for k in range(len(pieces))]

                    def counts(ph, k, pieces=pieces, starts=starts):
                        n, per, banks = pieces[k]
                        for j in range(n):
                            a, o = divmod(j, per)
                            c = (starts[k] + j) * P
                            last = nc.tensor.matmul(acc[0:P, banks[ph % 2] + a, o * P:(o + 1) * P],
                                                    c3[ph].bitcast(F8)[0:P, c:c + P], ident16[0:P, 0:P], start=True, stop=True)
                        last.then_inc(c3_mm[k], 1)

                    def landed(b, ph, w=w):
                        before = 16 * w * ((H - 1) // 4 + (ph == 0))
                        pe.wait_ge(c3_loaded[ph], (b // 4 * 16 if isinstance(b, int) else (b - ph) * 4) + (16 + before))

                    def body(b, ph, w=w, pieces=pieces, starts=starts, counts=counts, landed=landed):
                        for k, (n, per, banks) in enumerate(pieces):
                            pe.wait_ge(e3_ready[k], b + (H * w + 1))
                            ahead = 2 if banks[0] != banks[1] else 1
                            more = not isinstance(b, int) or b + ahead < H
                            for j in range(n):
                                if j == n - 1 and more:
                                    pe.wait_ge(piece_max[k], b + (H * w + 1))
                                    landed(b + ahead, (ph + ahead) % 4)
                                a, o = divmod(starts[k] + j, 3)
                                c = (starts[k] + j) * P
                                last = nc.tensor.matmul(acc[0:P, a, o * (D + 1):(o + 1) * (D + 1)], e3[ph % 2][:, c:c + P],
                                                        hN[:, bass.ds(b, 1), 0:D + 1].rearrange("p a d -> p (a d)"),
                                                        start=False, stop=False, skip_group_check=True)
                            if k == len(pieces) - 1:
                                last.then_inc(e3_used, 1)
                            if more:
                                counts((ph + ahead) % 4, k)
                    if w:
                        for k in range(len(SWEEPS[w - 1][1])):
                            pe.wait_ge(piece_max[k], H * w)
                    for k, (n, per, banks) in enumerate(pieces):
                        for b in range(2 if banks[0] != banks[1] else 1):
                            landed(b, b)
                            counts(b, k)
                    if w:
                        pe.wait_ge(sweep_out, w)
                    for a in range(SUM_BANKS):
                        m = min(3, nblk - 3 * a) * (D + 1)
                        nc.tensor.matmul(acc[0:P, a, 0:m], zero3[0:P, 0:P], zero3[0:P, 0:m], start=True, stop=False)
                    block_fours(pe, body)
                    for a in range(SUM_BANKS):
                        m = min(3, nblk - 3 * a) * (D + 1)
                        last = nc.tensor.matmul(acc[0:P, a, 0:m], zero3[0:P, 0:P], zero3[0:P, 0:m], start=False, stop=True)
                    last.then_inc(sweep_done, 1)
            with pe.If(fast < 1):
                pe.wait_ge(logits_out, 1)
                pe.wait_ge(prepared["layer3"], 1)
                scatter("rowsum")
                pe.wait_ge(scatter_out["rowsum"], NQ)
                scatter("agg3")
                for q, (c0, cw) in enumerate(GROUPS):
                    pe.wait_ge(scatter_out["agg3"], q + 1)
                    nc.tensor.matmul(acc[:, q, 0:cw], W3[:], aggT[:, c0:c0 + cw], start=True, stop=True).then_inc(lin3_done, 1)
                for q, (c0, cw) in enumerate(GROUPS):
                    pe.wait_ge(y3_ready, q + 1)
                    for j, b in enumerate(BLOCKS[q]):
                        last = nc.tensor.transpose(acc[0:P, q, j * D:(j + 1) * D], yT[:, b * P:(b + 1) * P], ident[:])
                    last.then_inc(back3_done, 1)

            def normalised(q, c0, cw):
                if q < DQ:
                    pe.wait_ge(x3_ready, q + 1)
                else:
                    pe.wait_ge(x3_late, q + 1 - DQ)
                for j, b in enumerate(BLOCKS[q]):
                    last = nc.tensor.transpose(acc[:, q, j * P:(j + 1) * P], x3[:, b, :], ident[0:P, 0:P])
                return last
            fill("fwd3n", normalised)
            to_nodes("back4", yT)

        @block.scalar
        def _(act):
            def relus(name, to, bias):
                for q, c0, cw in shares(name, ev_act):
                    act.wait_ge(mm_done, filled(name, q))
                    nc.scalar.activation(to[:, c0:c0 + cw], acc[:, q, 0:cw], ACT.Relu, bias=bias).then_inc(ev_act, 1)

            def copies(name, to, rows=128, bias=None):
                for q, c0, cw in shares(name, ev_act):
                    act.wait_ge(mm_done, filled(name, q))
                    if bias is None:
                        ins = nc.scalar.copy(to[:, c0:c0 + cw], acc[0:rows, q, 0:cw])
                    else:
                        ins = nc.scalar.activation(to[:, c0:c0 + cw], acc[0:rows, q, 0:cw], ACT.Identity, bias=bias)
                    ins.then_inc(ev_act, 1)

            def roots(n):
                act.wait_ge(var_ready, n)
                nc.scalar.activation(rstd[:], mv[:, :, 1], ACT.Sqrt, bias=eps[0:P, :]).then_inc(std_ready, 1)

            def normalise(name, n, to):
                roots(n)
                act.wait_ge(bias_ready, n)
                for q, c0, cw in shares(name, ev_act):
                    for j, b in enumerate(BLOCKS[q]):
                        last = nc.scalar.activation(to[:, b, :], acc[0:P, q, j * D:(j + 1) * D], ACT.Identity,
                                                    bias=shift[:, b:b + 1], scale=rstd[:, b:b + 1])
                    last.then_inc(ev_act, 1)

            def x_out(k):
                c0, cw = GROUPS[k]
                act.wait_ge(xt_mm, k + 1)
                nc.scalar.copy(xT[:, c0:c0 + cw], acc[:, 6, 0:cw]).then_inc(xt_out, 1)

            for q, (c0, cw) in enumerate(GROUPS):
                act.wait_ge(first_mm, q + 1)
                nc.scalar.copy(frow[:, c0:c0 + cw], acc[0:P, q, 0:cw]).then_inc(first_out, 1)

            act.wait_ge(first_out, NQ)
            act.wait_ge(count_bias, 1)
            for t in ACT_TILES:
                nc.scalar.activation(hid2[1][0:P, :], frow, ACT.Sign, scale=-1.0, bias=thr_bias[:, t:t + 1],
                                     accum_out=small[0:P, t:t + 1]).then_inc(counted, 1)
                act.wait_ge(counted, ACT_TILES.index(t) + 1)

            n = 0
            for k in range(4):
                for t in range(GT):
                    act.wait_ge(turned, n + 1)
                    nc.scalar.copy(keys[k][:, t * P * WC:(t + 1) * P * WC].rearrange("p (g h) -> p h g", h=WC),
                                   acc[:, n % 8, 0:WC * P].rearrange("p (h g) -> p h g", h=WC)).then_inc(turned_out, 1)
                    n += 1

            def turn_out(k, to, n, products, bank=6):
                c0, cw = GROUPS[k]
                act.wait_ge(wt_done, n + 1)
                act.wait_ge(prod_done, products + 1)
                nc.scalar.copy(to[:, 0:cw], acc[0:P, bank, 0:cw]).then_inc(wblk_ready, 1)

            def body(p, qp, blocks):
                units = blocks * UNITS
                first = isinstance(p, int) and p == 0
                for u in range(units):
                    up = u % 2
                    for t in turns_in(units, u):
                        if first and t % 2 == 0:
                            x_out(t // 2)
                        if not first:
                            turn_out(t // 2, wblk[t // 2 % 2][t % 2], TURNS * (p - 1) + t, NQ * (p - 1) + max(0, t // 2 - 1))
                    w = u // UNITS
                    if u % UNITS == 0:
                        wait(act, c_stored[w], p * 16)
                        if u == 0 and not (isinstance(p, int) and p < 2):
                            act.wait_ge(wt_done, TURNS * (p - 1))
                    act.wait_ge(unit_mm, p * (2 * UNITS) + u + 1)
                    for to, bank, scale in ((strip[qp][w], 1, 1.0 / WS_), (c_stage[w].bitcast(F8)[0:P], 0, CS)):
                        o = u % UNITS * UG * GD
                        extra = {"saturate": False} if bank == 0 else {}
                        nc.scalar.activation(to[:, :, o:o + 4 * GD].rearrange("p h (j l) -> p h j l", j=4),
                                             acc[0:P, 3 * up + bank, 0:4 * KW].rearrange("p (j h l) -> p h j l", j=4, l=GD),
                                             ACT.Copy, scale=scale, **extra)
                        last = nc.scalar.activation(to[:, :, o + 4 * GD:o + 5 * GD],
                                                    acc[0:P, 3 * up + 2, bank * KW:(bank + 1) * KW].rearrange("p (h l) -> p h l", l=GD),
                                                    ACT.Copy, scale=scale, **extra)
                    last.then_inc(unit_out, 1)
            fast0 = takes(act, FAST0)
            with act.If(fast0 > 0):
                act.wait_ge(stage_clear, 1)
                each_pair(act, body)
                for k in range(NQ):
                    turn_out(k, wblk[k % 2][0], TURNS * PAIRS + k, NQ * PAIRS + max(0, k - 1), tail_banks(k)[0])
            with act.If(fast0 < 1):
                for k in range(NQ):
                    x_out(k)

            normalise("back0", 1, x)
            copies("fwd1", xT)
            act.wait_ge(loaded, 16 * len(loads) + 1)
            relus("lin1", yT, BS[:])
            normalise("back1", 2, x)
            copies("fwd2", xT)
            for k in range(HALVES):
                relus(f"l2h{k}", hidden[:, k], BL[:, k:k + 1])
            for k in range(HALVES):
                relus(f"l2m{k}", hid2[k], BM1[:, k:k + 1])
            normalise("back2", 3, x)
            copies("fwd3", xT)
            copies("h3", hidden[:, 0], bias=B3[:])
            copies("arow", arow, rows=P)
            fast = takes(act, FAST)
            act.wait_ge(scalars_ready, 1)
            act.wait_ge(*emptied("arow", NQ - 1))
            with act.If(fast > 0):
                nc.scalar.activation(kj, bj, ACT.Exp).then_inc(exps_ready, 1)
                nc.scalar.activation(evj, vj, ACT.Exp)
                nc.scalar.activation(urow, arow, ACT.Exp, scale=1.0 - ALPHA, bias=small[0:P, 24:25]).then_inc(exps_ready, 1)
                act.wait_ge(exps_ready, 2)
                nc.scalar.mul(nkj, kj, -1.0).then_inc(exps_ready, 1)
                act.wait_ge(exps_ready, 3)
            act.wait_ge(l3_ready, 1)
            with act.If(fast > 0):
                for w, (first, pieces) in enumerate(SWEEPS):
                    nblk = sum(n for n, _, _ in pieces)
                    def body(b, ph, w=w, first=first, pieces=pieces, nblk=nblk):
                        if not isinstance(b, int) or b > 1:
                            for k in range(len(pieces)):
                                act.wait_ge(e3_ready[k], b + (H * w - 1))
                        elif w:
                            for k in range(len(SWEEPS[w - 1][1])):
                                act.wait_ge(e3_ready[k], H * w)
                        nc.scalar.activation(relu3[ph % 2][:, 0:nblk * P], urow[:, first * P:(first + nblk) * P], ACT.Relu,
                                             bias=nkj[:, bass.ds(b, 1)], scale=evj[:, bass.ds(b, 1)]).then_inc(relu_ready, 1)
                    block_fours(act, body)
                    act.wait_ge(sweep_done, w + 1)
                    for a in range(SUM_BANKS):
                        m = min(3, nblk - 3 * a)
                        f = first + 3 * a
                        last = nc.scalar.copy(raw3[:, f:f + m, :].rearrange("p a b -> p (a b)"), acc[0:P, a, 0:m * (D + 1)])
                    last.then_inc(sweep_out, 1)
                act.wait_ge(eps_in, 1)
                nc.scalar.activation(rstd[:], s_node[:, :, 0], ACT.Exp, scale=-ALPHA, bias=small[0:P, 20:21]).then_inc(eps_out, 1)
            with act.If(fast < 1):
                act.wait_ge(logits_in, 1)
                nc.scalar.activation(e_e, z_e, ACT.Exp).then_inc(logits_out, 1)
            roots(4)
            act.wait_ge(bias_ready, 4)
            for q in range(DQ, NQ):
                for b in BLOCKS[q]:
                    last = nc.scalar.activation(x3[:, b, :], x3[:, b, :], ACT.Identity, bias=shift[:, b:b + 1], scale=rstd[:, b:b + 1])
                last.then_inc(x3_late, 1)
            for q, (c0, cw) in enumerate(GROUPS):
                c = slice(c0, c0 + cw)
                act.wait_ge(elu_in, q + 1)
                nc.scalar.activation(aggT[:, c], yT[:, c], ACT.Relu, scale=-1.0).then_inc(elu_min, 1)
                act.wait_ge(elu_min, q + 1)
                nc.scalar.activation(aggT[:, c], aggT[:, c], ACT.Exp, scale=-1.0).then_inc(elu_exp, 1)
            normalise("back4", 5, x)


        @block.vector
        def _(dve):
            at_chain = [dve_chain, 0]

            def link(ins):
                at_chain[1] += 1
                ins.then_inc(at_chain[0], 1)
                dve.wait_ge(*at_chain)

            branch_links = {key: 0 for key in branch_chain}

            @contextmanager
            def branch(flag, which, yes):
                outer = at_chain[:]
                at_chain[:] = [branch_chain[which, yes], branch_links[which, yes]]
                with dve.If(flag > 0 if yes else flag < 1):
                    yield
                branch_links[which, yes] = at_chain[1]
                at_chain[:] = outer

            def norm_stats(n, of):
                link(of())
                for b in range(H):
                    last = nc.vector.bn_aggr(mv[:, b, :], stats[:, b, :])
                last.then_inc(var_ready, 1)
                dve.wait_ge(std_ready, n)
                link(nc.vector.reciprocal(rstd[:], rstd[:]))
                nc.vector.scalar_tensor_tensor(out=shift[:], in0=mv[:, :, 0], scalar=-1.0, in1=rstd[:],
                                               op0=ALU.mult, op1=ALU.mult).then_inc(bias_ready, 1)
                dve.wait_ge(bias_ready, n)

            def layer_norm(name, n, to):
                def of():
                    for q in range(NQ):
                        dve.wait_ge(mm_done, filled(name, q))
                        for j, b in enumerate(BLOCKS[q]):
                            last = nc.vector.bn_stats(stats[:, b, :], acc[0:P, q, j * D:(j + 1) * D])
                    return last
                norm_stats(n, of)
                for q, c0, cw in shares(name, ev_dve):
                    for j, b in enumerate(BLOCKS[q]):
                        last = nc.vector.tensor_scalar(to[:, b, :], acc[0:P, q, j * D:(j + 1) * D], mv[:, b, 0:1],
                                                       rstd[:, b:b + 1], ALU.subtract, ALU.mult)
                    last.then_inc(ev_dve, 1)

            def relus(name, to, bias):
                for q, c0, cw in shares(name, ev_dve):
                    dve.wait_ge(mm_done, filled(name, q))
                    nc.vector.tensor_scalar(to[:, c0:c0 + cw], acc[:, q, 0:cw], bias, 0.0, ALU.add, ALU.max).then_inc(ev_dve, 1)

            def copies(name, to):
                for q, c0, cw in shares(name, ev_dve):
                    dve.wait_ge(mm_done, filled(name, q))
                    nc.vector.tensor_copy(to[:, c0:c0 + cw], acc[:, q, 0:cw]).then_inc(ev_dve, 1)

            def add_x(name, bias):
                for q, (c0, cw) in enumerate(GROUPS):
                    dve.wait_ge(mm_done, filled(name, q))
                    nc.vector.scalar_tensor_tensor(out=yT[:, c0:c0 + cw], in0=acc[:, q, 0:cw], scalar=bias,
                                                   in1=xT[:, c0:c0 + cw], op0=ALU.add, op1=ALU.add).then_inc(ev_dve, 1)

            nc.vector.memset(ones[:], 1.0)
            nc.vector.memset(ones16[:], 1.0)
            nc.vector.memset(eps[:], LN_EPS)
            nc.vector.memset(tmp2[:, 0:1], 0.0).then_inc(prod_done, 1)
            dve.wait_ge(consts_ready, 2)
            nc.vector.tensor_scalar(thr_bias, thr, -0.5, None, ALU.add).then_inc(count_bias, 1)
            nc.vector.tensor_copy(ident16[:], ident[:])
            dve.wait_ge(dst_loaded, 16)
            firsts = tmp[0:P, 0:EC // ROWE]
            link(nc.vector.tensor_copy(firsts, dst_i[:].rearrange("p (k r) -> p k r", r=ROWE)[:, :, 0]))
            for k in range(EC // ROWE):
                last = nc.vector.tensor_scalar(diag[:, k * P:(k + 1) * P], ident[0:P, 0:P], firsts[:, k:k + 1], None, ALU.mult)
            last.then_inc(first_ready, 1)
            nc.vector.memset(aggT[:], 0.0).then_inc(prod_added, NQ)
            dve.wait_ge(first_out, NQ)

            def start(t, scale, shift_):
                link(nc.vector.tensor_scalar(small[0:P, 8 + t:9 + t], small[0:P, t:t + 1], scale, shift_, ALU.mult, ALU.add))
                link(nc.vector.tensor_scalar(small[0:P, 8 + t:9 + t], small[0:P, 8 + t:9 + t], 0.0, float(NROW - 1), ALU.max, ALU.min))
                nc.vector.tensor_scalar(start_i[:, t:t + 1], small[0:P, 8 + t:9 + t], float(ROWE), None, ALU.mult).then_inc(starts_ready, 1)
            count = None
            for t in TILE_ORDER:
                if count is None or t not in ACT_TILES and count[0] != t:
                    u = [v for v in TILE_ORDER if v not in ACT_TILES and (count is None or v > count[0])][0]
                    count = (u, link(nc.vector.tensor_scalar(diag[:, :], frow[:, :], thr[:, u:u + 1], None, ALU.is_lt, ALU.add,
                                                             accum_out=small[0:P, u:u + 1])))
                if t in ACT_TILES:
                    dve.wait_ge(counted, ACT_TILES.index(t) + 1)
                    start(t, 0.5, N / 2 - 1.0)
                else:
                    start(t, 1.0, -1.0)
            dve.wait_ge(windows_in, 16 * 2 * GT)
            c_lo, c_key, c_wh, c_wl, c_a, c_b = cut
            dve.wait_ge(edges_loaded, 32)

            def note(s_):
                nc.vector.tensor_copy(tmp2[:, 0:1], ones[:, 0:1]).then_inc(s_, 1)
            link(nc.vector.tensor_copy(c_a, win_i[0]))
            link(nc.vector.tensor_scalar(c_b, c_a, 1.0 / P, -0.5 + 0.5 / P, ALU.mult, ALU.add))
            link(nc.vector.tensor_scalar(c_lo, c_b, ROUND, None, ALU.add))
            link(nc.vector.tensor_scalar(c_b, c_lo, -ROUND, None, ALU.add))
            link(nc.vector.scalar_tensor_tensor(out=c_lo, in0=c_b, scalar=-float(P), in1=c_a, op0=ALU.mult, op1=ALU.add))
            note(cut_ready)
            link(nc.vector.tensor_copy(c_a, win_i[1]))
            for t in range(GT):
                last = nc.vector.tensor_scalar(within[:, t, :], c_a[:, t, :], thr[:, t:t + 1], None, ALU.subtract)
            link(last)
            link(nc.vector.tensor_scalar(c_wh, within, float(GD - 1), None, ALU.is_le))
            link(nc.vector.scalar_tensor_tensor(out=c_a, in0=within, scalar=0.0, in1=c_wh, op0=ALU.is_ge, op1=ALU.mult,
                                                accum_out=small[0:P, 16:17]))
            link(nc.vector.scalar_tensor_tensor(out=c_wh, in0=c_b, scalar=float(GD), in1=within, op0=ALU.mult, op1=ALU.add))
            link(nc.vector.scalar_tensor_tensor(out=c_key, in0=c_wh, scalar=KEY0, in1=c_a, op0=ALU.add, op1=ALU.mult))
            note(cut_ready)
            w16 = win_i[0].rearrange("p a b -> p (a b)").bitcast(F16)[:, 0:GT * WIN].rearrange("p (a b) -> p a b", a=GT)
            dve.wait_ge(weights_in, 16 * GT)
            link(nc.vector.tensor_scalar(w16, win_w, WS_, None, ALU.mult))
            link(nc.vector.tensor_copy(c_wh, w16))
            note(cut_ready)
            link(nc.vector.scalar_tensor_tensor(out=c_wl, in0=win_w, scalar=WS_, in1=c_wh, op0=ALU.mult, op1=ALU.subtract))
            note(cut_ready)
            w16l = win_i[1].rearrange("p a b -> p (a b)").bitcast(F16)[:, 0:GT * WIN].rearrange("p (a b) -> p a b", a=GT)
            link(nc.vector.tensor_copy(w16l, c_wl))
            link(nc.vector.tensor_tensor(c_a, c_wl, w16l, ALU.subtract))
            nc.vector.tensor_scalar(c_b, c_a, 0.0, None, ALU.is_equal, ALU.add, accum_out=small[0:P, 17:18]).then_inc(flag_sums, 1)
            dve.wait_ge(turned_out, 4 * GT)
            dve.wait_ge(consts_ready, 3)
            dve.wait_ge(flag_mm, 1)
            link(nc.vector.tensor_scalar(small[:, 18:19], acc[:, 0, 0:1], float(E), None, ALU.is_equal))
            link(nc.vector.tensor_scalar(small[:, 19:20], acc[:, 0, 1:2], float(P * GT * WIN), None, ALU.is_equal))
            nc.vector.tensor_tensor(flag_i[:, FAST0:FAST0 + 1], small[:, 18:19], small[:, 19:20], ALU.mult).then_inc(fast0_ready, 1)
            fast0 = takes(dve, FAST0)

            def prepare(stage):
                nc.vector.memset(zeros, 0.0)
                nc.vector.memset(ones_e, 1.0)
                nc.vector.tensor_copy(src_f, src_i[:])
                link(nc.vector.tensor_copy(dst_f, dst_i[:]))
                nc.vector.tensor_copy(tmp2[:, 0:1], ones[:, 0:1]).then_inc(prepared[stage], 1)

            def scatter(name, values, key):
                with dve.Fori(0, EC // 2) as i:
                    for k in range(2):
                        dve.wait_ge(chunk_done[name], i * 2 + (k + 1))
                        nc.vector.tensor_scalar(onehot[k], node_iota, key[:, bass.ds(i * 2 + k, 1)], None, ALU.is_equal)
                        if name in gathered:
                            dve.wait_ge(gathered[name][k], i * 16 + 16)
                        nc.vector.tensor_scalar(msg[k], rows_g[k] if name in gathered else ones[0:P, :],
                                                values[:, bass.ds(i * 2 + k, 1)], None, ALU.mult
                                                ).then_inc(msg_ready[name], 1)

            def scattered(name, to):
                for q, (c0, cw) in enumerate(GROUPS):
                    dve.wait_ge(scatter_done[name], q + 1)
                    to(slice(c0, c0 + cw), acc[:, q, 0:cw]).then_inc(scatter_out[name], 1)
                dve.wait_ge(scatter_out[name], NQ)

            def mean(c, bank):
                return nc.vector.tensor_tensor(aggT[:, c], bank, normT[:, c], ALU.mult)

            def marked(s_):
                nc.vector.tensor_copy(tmp2[:, 0:1], ones[:, 0:1]).then_inc(s_, 1)

            def hots(U, up):
                wait(dve, unit_mm, U - 1)
                lo, key, loh, lol = hot[up]
                o = bass.ds(U * UC, UC)

                def wide_(k, n):
                    return keys[k][:, o].unsqueeze(1).broadcast_to([128, n, UC])
                nc.vector.tensor_tensor(lo, iota_lo, wide_(0, P), ALU.is_equal).then_inc(lo_ready, 1)
                nc.vector.tensor_tensor(key, iota_key, wide_(1, KW), ALU.is_equal)
                dve.wait_ge(lo_ready, U + 1)
                nc.vector.tensor_tensor(loh, lo, wide_(2, P), ALU.mult)
                nc.vector.tensor_tensor(lol, lo, wide_(3, P), ALU.mult).then_inc(hot_ready, 1)

            def degrees(t):
                for l in range(GD):
                    last = nc.vector.tensor_scalar(tmp[0:P, 0:WIN] if l % 2 else tmp2[0:P, 128:128 + WIN], within[:, t, :],
                                                   float(l), None, ALU.is_equal, ALU.add, accum_out=ideg[:, t * GD + l:t * GD + l + 1])
                    if l % 2 or l == GD - 1:
                        link(last)
                link(nc.vector.tensor_scalar(ideg[:, t * GD:(t + 1) * GD], ideg[:, t * GD:(t + 1) * GD], 1.0, None, ALU.max))

            def add_product(k, p, bank=7):
                m = NQ * p + k
                c0, cw = GROUPS[k]
                dve.wait_ge(prod_done, m + 2)
                dve.wait_ge(prod_added, m + 1)
                nc.vector.tensor_tensor(aggT[:, c0:c0 + cw], aggT[:, c0:c0 + cw], acc[:, bank, 0:cw], ALU.add).then_inc(prod_added, 1)

            with branch(fast0, FAST0, True):
                hots(0, 0)

                def body(p, qp, blocks):
                    units = blocks * UNITS
                    for u in range(units):
                        if blocks == 2 or u < units - 1:
                            hots(p * (2 * UNITS) + u + 1, (u + 1) % 2)
                        if not (isinstance(p, int) and p == 0):
                            for k in adds_in(units, u):
                                add_product(k, p - 1)
                        if blocks == 1:
                            degrees(u)
                            if u == units - 1:
                                nc.vector.reciprocal(ideg[:], ideg[:]).then_inc(deg_ready, 1)
                each_pair(dve, body)
                for k in range(NQ):
                    add_product(k, PAIRS, tail_banks(k)[1])
                dve.wait_ge(prod_added, NQ * (PAIRS + 2))
                marked(sums_ready)
            with branch(fast0, FAST0, False):
                dve.wait_ge(node_iota_ready["layer0"], 1)
                prepare("layer0")
                scatter("agg0", w_e, src_f)
                scattered("agg0", lambda c, bank: nc.vector.tensor_copy(aggT[:, c], bank))
                marked(sums_ready)

            dve.wait_ge(loaded, 16 * len(loads))
            nc.vector.tensor_tensor(BS[:], BS[:], BN_[:], ALU.add).then_inc(loaded, 1)
            nc.vector.tensor_copy(A3S[:], A3[:, 0:1].broadcast_to([D, 128]))
            add_x("lin0", B0[:])
            layer_norm("back0", 1, x)

            def parts(name):
                for i in range(NX):
                    last_q = min(NQ - 1, (i + 1) * XC // QB - 1)
                    for q in (last_q, last_q - 1):
                        dve.wait_ge(*emptied(name, q))
                    c = slice(i * XC, min(H, (i + 1) * XC))
                    link(nc.vector.tensor_scalar(x16[0][:, c, :], x[:, c, :], XS, None, ALU.mult))
                    nc.vector.scalar_tensor_tensor(out=x16[1][:, c, :].rearrange("p a b -> p (a b)"),
                                                   in0=x[:, c, :].rearrange("p a b -> p (a b)"), scalar=XS,
                                                   in1=x16[0][:, c, :].rearrange("p a b -> p (a b)"),
                                                   op0=ALU.mult, op1=ALU.subtract).then_inc(x16_ready, 1)

            def means(layer):
                for q, (c0, cw) in enumerate(GROUPS):
                    n = NQ * layer + q
                    c = slice(c0, c0 + cw)
                    dve.wait_ge(dense_mm, n + 1)
                    nc.vector.scalar_tensor_tensor(out=aggT[:, c], in0=acc[:, n % 2, 0:cw], scalar=1.0 / (CS * XS), in1=normT[:, c],
                                                   op0=ALU.mult, op1=ALU.mult, accum_out=small[:, 57 + q:58 + q]).then_inc(dense_out, 1)
            with branch(fast0, FAST0, True):
                dve.wait_ge(c_stored[0], 16 * (H // 2 + 1))
                dve.wait_ge(c_stored[1], 16 * (H // 2))
                parts("back0")
            all_emptied(dve, "back0")
            marked(x_new)
            nc.vector.memset(small[:, 21:22], 0.0)
            with branch(fast0, FAST0, True):
                dve.wait_ge(deg_loaded, 16)
                means(0)
                dve.wait_ge(dense_out, NQ)
                link(nc.vector.tensor_reduce(small[:, 20:21], small[:, 57:57 + NQ], AX_X, ALU.add))
                link(nc.vector.tensor_tensor(small[:, 20:21], small[:, 20:21], small[:, 20:21], ALU.subtract))
                link(nc.vector.tensor_scalar(small[:, 21:22], small[:, 20:21], 0.0, None, ALU.is_equal))
            link(nc.vector.tensor_copy(tmp2[:, 1:2], ones[:, 0:1]))
            nc.vector.tensor_copy(flag_i[:, FAST:FAST + 1], small[:, 21:22]).then_inc(fast_ready, 1)
            fast = takes(dve, FAST)
            with branch(fast, FAST, True):
                marked(sums_ready)
            with branch(fast, FAST, False):
                dve.wait_ge(node_iota_ready["layers12"], 1)
                prepare("layers12")
                scatter("deg", ones_e, dst_f)
                scattered("deg", lambda c, bank: nc.vector.tensor_scalar(normT[:, c], bank, 1.0, None, ALU.max))
                link(nc.vector.reciprocal(normT[:], normT[:]))
                scatter("agg1", ones_e, dst_f)
                scattered("agg1", mean)
                marked(sums_ready)
            for q, (c0, cw) in enumerate(GROUPS):
                dve.wait_ge(*emptied("lin1", q))
                nc.vector.tensor_tensor(yT[:, c0:c0 + cw], yT[:, c0:c0 + cw], xT[:, c0:c0 + cw], ALU.add).then_inc(y1_ready, 1)
            layer_norm("back1", 2, x)
            with branch(fast, FAST, True):
                parts("back1")
            all_emptied(dve, "back1")
            marked(x_new)
            with branch(fast, FAST, True):
                means(1)
                dve.wait_ge(dense_out, 2 * NQ)
                marked(sums_ready)
            with branch(fast, FAST, False):
                scatter("agg2", ones_e, dst_f)
                scattered("agg2", mean)
                marked(sums_ready)
            for k in range(HALVES):
                relus(f"l2h{k}", hidden[:, k], BL[:, k:k + 1])
            for k in range(HALVES):
                relus(f"l2m{k}", hid2[k], BM1[:, k:k + 1])
            add_x("l2o", BM2[:])
            layer_norm("back2", 3, x)
            all_emptied(dve, "back2")
            marked(x_new)
            copies("fwd3", xT)
            for q, c0, cw in shares("h3", ev_dve):
                dve.wait_ge(mm_done, filled("h3", q))
                nc.vector.tensor_scalar(hidden[:, 0, c0:c0 + cw], acc[:, q, 0:cw], B3[:], None, ALU.add).then_inc(ev_dve, 1)
            for q in range(NQ):
                dve.wait_ge(mm_done, filled("s3", q))
                nb = len(BLOCKS[q])
                nc.vector.tensor_copy(s_node[:, q * QB:q * QB + nb, :].rearrange("p h k -> p (h k)"),
                                      acc[0:P, q, 0:2 * nb]).then_inc(ev_dve, 1)
            s = lambda k: small[0:P, k:k + 1]
            dve.wait_ge(*emptied("s3", NQ - 1))
            link(nc.vector.tensor_copy(sd, s_node[:, :, 1]))
            nc.vector.tensor_reduce(s(4), sd, AX_X, ALU.max)
            nc.vector.tensor_reduce(s(6), s_node[:, :, 0], AX_X, ALU.max)
            link(nc.vector.tensor_reduce(s(5), sd, AX_X, ALU.min))
            nc.vector.tensor_scalar(s(5), s(5), -1.0, None, ALU.mult).then_inc(max_in, 1)
            link(nc.vector.memset(zero3, 0.0))
            with branch(fast, FAST, True):
                link(nc.vector.memset(smax, 0.0))
            dve.wait_ge(max_out, 1)
            MAXS, NMINS, MAXA = s(8), s(9), s(10)
            link(nc.vector.tensor_tensor(s(12), MAXS, MAXA, ALU.add))
            link(nc.vector.tensor_scalar(s(13), s(12), 0.0, 1.0 - ALPHA, ALU.max, ALU.mult))
            link(nc.vector.scalar_tensor_tensor(out=s(14), in0=MAXS, scalar=ALPHA, in1=s(13), op0=ALU.mult, op1=ALU.add))
            link(nc.vector.tensor_scalar(bj, sd, ALPHA, s(14), ALU.mult, ALU.subtract))
            link(nc.vector.tensor_scalar(vj, sd, MAXA, 1.0 - ALPHA, ALU.add, ALU.mult))
            link(nc.vector.tensor_tensor(vj, vj, bj, ALU.add))
            nc.vector.tensor_scalar(s(24), MAXA, ALPHA - 1.0, None, ALU.mult)
            link(nc.vector.tensor_tensor(s(15), MAXS, NMINS, ALU.add))
            link(nc.vector.tensor_scalar(s(15), s(15), CS - 2.0, 1.0 / (CS - 2.0), ALU.max, ALU.mult))
            link(nc.vector.reciprocal(s(25), s(15)))
            link(nc.vector.tensor_tensor(s(26), NMINS, s(25), ALU.mult))
            link(nc.vector.tensor_scalar(s(26), s(26), 1.0, None, ALU.add))
            link(nc.vector.tensor_scalar(s(27), s(15), -1.0, None, ALU.mult))
            nc.vector.tensor_scalar(sp_, sd, s(25), s(26), ALU.mult, ALU.add).then_inc(scalars_ready, 1)
            nc.vector.memset(hN[:, :, D:D + 1], 1.0)
            for q, c0, cw in shares("hnode", ev_dve):
                dve.wait_ge(mm_done, filled("hnode", q))
                nb = len(BLOCKS[q])
                nc.vector.tensor_copy(hN[:, q * QB:q * QB + nb, 0:D],
                                      acc[0:P, q, 0:nb * D].rearrange("p (j d) -> p j d", d=D)).then_inc(ev_dve, 1)
            all_emptied(dve, "arow")
            all_emptied(dve, "hnode")
            nc.vector.tensor_copy(tmp2[:, 0:1], ones[:, 0:1]).then_inc(l3_ready, 1)
            dve.wait_ge(l3_ready, 1)
            with branch(fast, FAST, True):
                dve.wait_ge(exps_ready, 3)
                for w, (first, pieces) in enumerate(SWEEPS):
                    def body(b, ph, w=w, first=first, pieces=pieces):
                        par = ph % 2
                        older = H * w if isinstance(b, int) and b < 2 else b + (H * w - 1)
                        at_ = 0
                        for k, (n, per, banks) in enumerate(pieces):
                            if k == 0:
                                dve.wait_ge(relu_ready, b + (H * w + 1))
                                wait(dve, e3_used, older)
                            dve.wait_ge(c3_mm[k], b + (H * w + 1))
                            wait(dve, piece_max[k], b + H * w)
                            lanes = slice(at_ * P, (at_ + n) * P)

                            def by_bank(t, per=per):
                                return t.rearrange("p (a c) -> p a c", c=per * P) if n > per else t
                            bank = banks[par]
                            of = acc[0:P, bank:bank + n // per, 0:per * P] if n > per else acc[0:P, bank, 0:n * P]
                            nc.vector.scalar_tensor_tensor(out=by_bank(e3[par][:, lanes]), in0=by_bank(relu3[par][:, lanes]),
                                                           scalar=kj[:, bass.ds(b, 1)], in1=of, op0=ALU.add, op1=ALU.mult
                                                           ).then_inc(e3_ready[k], 1)
                            c0 = (first + at_) * P
                            r = by_bank(smax[:, c0:c0 + n * P])
                            nc.vector.scalar_tensor_tensor(out=r, in0=of, scalar=sp_[:, bass.ds(b, 1)], in1=r, op0=ALU.min, op1=ALU.max
                                                           ).then_inc(piece_max[k], 1)
                            at_ += n
                    block_fours(dve, body)
                for k in range(2):
                    dve.wait_ge(piece_max[k], H * (1, NS)[k == 0])
                rows = tmp[0:P, 0:H]
                link(nc.vector.tensor_scalar(urow, smax, 0.5, -BIG, ALU.is_lt, ALU.mult))
                link(nc.vector.scalar_tensor_tensor(out=smax, in0=smax, scalar=s(15), in1=urow, op0=ALU.mult, op1=ALU.add))
                link(nc.vector.tensor_tensor_reduce(urow, smax, arow, 1.0, -2.0 * BIG, ALU.add, ALU.max, s(2)))
                nc.vector.scalar_tensor_tensor(out=s(2), in0=s(26), scalar=s(27), in1=s(2), op0=ALU.mult, op1=ALU.add).then_inc(max_in, 1)
                dve.wait_ge(max_out, 2)
                link(nc.vector.scalar_tensor_tensor(out=s(17), in0=s(3), scalar=ALPHA, in1=s(3), op0=ALU.mult, op1=ALU.max))
                link(nc.vector.scalar_tensor_tensor(out=s(18), in0=MAXA, scalar=ALPHA, in1=s(17), op0=ALU.mult, op1=ALU.add))
                link(nc.vector.scalar_tensor_tensor(out=s(19), in0=s(12), scalar=ALPHA, in1=s(12), op0=ALU.mult, op1=ALU.max))
                nc.vector.tensor_tensor(s(20), s(18), s(19), ALU.subtract).then_inc(eps_in, 1)
                dve.wait_ge(eps_out, 1)
                dve.wait_ge(sweep_out, NS)
                link(nc.vector.scalar_tensor_tensor(out=rows, in0=rstd[:], scalar=SUM_EPS * CS, in1=raw3[:, :, D], op0=ALU.mult, op1=ALU.add))
                link(nc.vector.reciprocal(rows, rows))
                for b in range(H):
                    last = nc.vector.scalar_tensor_tensor(out=x3[:, b, :], in0=raw3[:, b, 0:D], scalar=rows[:, b:b + 1],
                                                          in1=x[:, b, :], op0=ALU.mult, op1=ALU.add)
                link(last)

            with branch(fast, FAST, False):
                prepare("layer3")
                link(nc.vector.tensor_copy(tmp2[:, 1:2], ones[:, 0:1]))
                nc.vector.tensor_copy(tmp2[:, 0:1], ones[:, 0:1]).then_inc(s_col_done, 2)
                for n in range(2):
                    with dve.Fori(0, EC // 2) as i:
                        for k in range(2):
                            dve.wait_ge(gathered[f"s{n}"][k], i * 16 + 16)
                            nc.vector.tensor_copy(s_of[n][:, bass.ds(i * 2 + k, 1)], srow[k][:, 1 - n:2 - n]).then_inc(s_col_done, 1)
                dve.wait_ge(s_col_done, 2 * EC + 2)
                link(nc.vector.tensor_tensor(s_of[0], s_of[0], s_of[1], ALU.add))
                link(nc.vector.scalar_tensor_tensor(out=z_e, in0=s_of[0], scalar=ALPHA, in1=s_of[0], op0=ALU.mult, op1=ALU.max))
                nc.vector.tensor_reduce(s(22), z_e, AX_X, ALU.max).then_inc(general_max, 1)
                dve.wait_ge(general_gmax, 1)
                nc.vector.tensor_scalar(z_e, z_e, s(23), None, ALU.subtract).then_inc(logits_in, 1)
                dve.wait_ge(logits_out, 1)
                dve.wait_ge(node_iota_ready["layer3"], 1)
                scatter("rowsum", e_e, src_f)
                scattered("rowsum", lambda c, bank: nc.vector.tensor_copy(normT[:, c], bank))
                scatter("agg3", e_e, src_f)
                scattered("agg3", lambda c, bank: nc.vector.tensor_copy(aggT[:, c], bank))
                for q, (c0, cw) in enumerate(GROUPS):
                    c = slice(c0, c0 + cw)
                    link(nc.vector.tensor_scalar(tmp[:, 0:cw], normT[:, c], SUM_EPS, None, ALU.add))
                    link(nc.vector.reciprocal(tmp2[:, 0:cw], tmp[:, 0:cw]))
                    dve.wait_ge(lin3_done, q + 1)
                    link(nc.vector.scalar_tensor_tensor(out=tmp[:, 0:cw], in0=normT[:, c], scalar=B3[:], in1=acc[:, q, 0:cw],
                                                        op0=ALU.mult, op1=ALU.add))
                    link(nc.vector.tensor_tensor(tmp[:, 0:cw], tmp[:, 0:cw], tmp2[:, 0:cw], ALU.mult))
                    nc.vector.tensor_tensor(yT[:, c], tmp[:, 0:cw], xT[:, c], ALU.add).then_inc(y3_ready, 1)
                    dve.wait_ge(y3_ready, q + 1)
                for q in range(NQ):
                    dve.wait_ge(back3_done, q + 1)
                    for j, b in enumerate(BLOCKS[q]):
                        last = nc.vector.tensor_copy(x3[:, b, :], acc[0:P, q, j * D:(j + 1) * D])
                link(last)

            def of():
                for b in range(H):
                    last = nc.vector.bn_stats(stats[:, b, :], x3[:, b, :])
                return last
            norm_stats(4, of)
            for q in range(DQ):
                for b in BLOCKS[q]:
                    last = nc.vector.tensor_scalar(x3[:, b, :], x3[:, b, :], mv[:, b, 0:1], rstd[:, b:b + 1], ALU.subtract, ALU.mult)
                last.then_inc(x3_ready, 1)

            def scaled(q):
                c0, cw = GROUPS[q]
                dve.wait_ge(mm_done, filled("fwd3n", q))
                nc.vector.tensor_scalar(yT[:, c0:c0 + cw], acc[:, q, 0:cw], G3[:], BE3[:], ALU.mult, ALU.add).then_inc(elu_in, 1)
            scaled(0)
            for q, (c0, cw) in enumerate(GROUPS):
                c = slice(c0, c0 + cw)
                if q + 1 < NQ:
                    scaled(q + 1)
                dve.wait_ge(elu_exp, q + 1)
                link(nc.vector.scalar_tensor_tensor(out=yT[:, c], in0=yT[:, c], scalar=0.0, in1=aggT[:, c],
                                                    op0=ALU.max, op1=ALU.add))
                nc.vector.scalar_tensor_tensor(out=yT[:, c], in0=yT[:, c], scalar=-1.0, in1=xT[:, c],
                                               op0=ALU.add, op1=ALU.add).then_inc(ev_dve, 1)
            layer_norm("back4", 5, x)
            all_emptied(dve, "back4")
            marked(x_new)
_INS = ["x", "src", "dst", "edge_weight", "L0_gnn_weight", "L0_gnn_bias", "L1_gnn_W_self", "L1_gnn_b_self",
        "L1_gnn_W_nei", "L1_gnn_b_nei", "L2_gnn_W_l", "L2_gnn_b_l", "L2_gnn_W_r", "L2_gnn_Wm1", "L2_gnn_bm1",
        "L2_gnn_Wm2", "L2_gnn_bm2", "L3_gnn_W", "L3_gnn_a", "L3_gnn_bias", "L3_gnn_gamma", "L3_gnn_beta"]
_TRANSPOSED = ("L1_gnn_W_self", "L1_gnn_W_nei")


def kernel(**inputs):
    import numpy as np
    import concourse.bacc as bacc
    from concourse.bass_utils import run_bass_kernel_spmd

    nc = bacc.Bacc("TRN2", target_bir_lowering=False, num_devices=1)
    arrays, args = {}, []
    for name in _INS:
        a = np.asarray(inputs[name])
        a = np.ascontiguousarray(a.T if name in _TRANSPOSED else a)
        arrays[f"in_{name}"] = a
        args.append(nc.dram_tensor(f"in_{name}", a.shape, mybir.dt.from_np(a.dtype), kind="ExternalInput").ap())
    out = nc.dram_tensor("out_x", inputs["x"].shape, F32, kind="ExternalOutput").ap()
    gnn_stack(nc, *args, out)
    r = run_bass_kernel_spmd(nc, [arrays], core_ids=[0])
    return r.results[0]["out_x"]
```
